# Optimizing a Trainium2 kernel written in Bass

```python
import numpy as np
import jax
import jax.numpy as jnp

def _softmax(x, axis=-1):
    return jax.nn.softmax(x, axis=axis)

def _gelu(x):
    return jax.nn.gelu(x, approximate=True)

def _silu(x):
    return jax.nn.silu(x)

def _sigmoid(x):
    return jax.nn.sigmoid(x)

def _layernorm(x, axis=-1, eps=1e-05):
    m = jnp.mean(x, axis=axis, keepdims=True)
    v = jnp.var(x, axis=axis, keepdims=True)
    return (x - m) / jnp.sqrt(v + eps)

def _scatter_add(tgt, idx, src, axis=0):
    return tgt.at[idx].add(src)

def _segment_sum(src, seg, n):
    return jax.ops.segment_sum(src, seg, n)
kernel_name = 'mk_gnn_resnorm_d1_gnn_r8_8cd8c2'

def setup_inputs(seed: int=0):
    np.random.seed(seed)
    _w = jnp.asarray

    def _rec_inputs():
        import jax
        import jax.numpy as jnp
        _gk = jax.random.key(seed)
        x = -0.000202 + 1 * jax.random.normal(jax.random.fold_in(_gk, 1), (6250, 128), jnp.float32)
        _s = jax.random.randint(jax.random.fold_in(_gk, 2), (100000,), 0, 6250, jnp.int32)
        _d = jax.random.randint(jax.random.fold_in(_gk, 3), (100000,), 0, 6250, jnp.int32)
        _loop = jnp.arange(6250, dtype=jnp.int32)
        src = jnp.concatenate([_s, _d, _loop])
        dst = jnp.concatenate([_d, _s, _loop])
        _o = jnp.argsort(dst, stable=True)
        src = src[_o]
        dst = dst[_o]
        edge_attr_128 = -6.47781e-05 + 0.999943 * jax.random.normal(jax.random.fold_in(_gk, 11), (206250, 128), jnp.float32)
        return (x, src, dst, edge_attr_128)
    x, src, dst, edge_attr_128 = _rec_inputs()

    def _L0_gnn_setup():
        import jax, jax.numpy as jnp
        import numpy as np
        N_NODES = 6250
        N_EDGES = 200000
        F = 128
        UNITS = 128

        def leaky_relu2(x):
            return jnp.where(x > 0, x, 0.2 * x)

        def glorot(key, shape):
            lim = np.sqrt(6.0 / (shape[0] + shape[1]))
            return jax.random.uniform(key, shape, jnp.float32, -lim, lim)
        key = jax.random.key(seed)
        ks = jax.random.split(key, 8)
        node = jax.random.normal(ks[0], (N_NODES, F), jnp.float32)
        edge = jax.random.normal(ks[1], (N_EDGES, F), jnp.float32)
        edge_index = jax.random.randint(ks[2], (N_EDGES, 2), 0, N_NODES, jnp.int64)
        W_lin = glorot(ks[3], (F, UNITS))
        b_lin = jnp.zeros((UNITS,), jnp.float32)
        W_att = glorot(ks[4], (2 * F, UNITS))
        b_att = jnp.zeros((UNITS,), jnp.float32)
        w_alpha = glorot(ks[5], (UNITS, 1))
        return {'node': node, 'edge': edge, 'edge_index': edge_index, 'W_lin': W_lin, 'b_lin': b_lin, 'W_att': W_att, 'b_att': b_att, 'w_alpha': w_alpha}
    _L0_gnn_all = _L0_gnn_setup()
    _L0_gnn_in = {k: v for k, v in _L0_gnn_all.items() if k in ('W_lin', 'b_lin', 'W_att', 'b_att', 'w_alpha')}
    del _L0_gnn_all
    return {'x': x, 'src': src, 'dst': dst, 'edge_attr_128': edge_attr_128, 'L0_gnn_W_lin': _L0_gnn_in['W_lin'], 'L0_gnn_b_lin': _L0_gnn_in['b_lin'], 'L0_gnn_W_att': _L0_gnn_in['W_att'], 'L0_gnn_b_att': _L0_gnn_in['b_att'], 'L0_gnn_w_alpha': _L0_gnn_in['w_alpha']}

def reference(x, src, dst, edge_attr_128, L0_gnn_W_lin, L0_gnn_b_lin, L0_gnn_W_att, L0_gnn_b_att, L0_gnn_w_alpha):
    import jax
    import jax.numpy as jnp

    def _L0_gnn_ref(node, edge, edge_index, W_lin, b_lin, W_att, b_att, w_alpha):
        import jax, jax.numpy as jnp
        import numpy as np
        N_NODES = 6250
        N_EDGES = 200000
        F = 128
        UNITS = 128

        def leaky_relu2(x):
            return jnp.where(x > 0, x, 0.2 * x)

        def glorot(key, shape):
            lim = np.sqrt(6.0 / (shape[0] + shape[1]))
            return jax.random.uniform(key, shape, jnp.float32, -lim, lim)
        recv = edge_index[:, 0]
        send = edge_index[:, 1]
        n_in = node[recv]
        n_out = node[send]
        wn_out = n_out @ W_lin + b_lin
        e_ij = leaky_relu2(jnp.concatenate([n_in, n_out], axis=-1) @ W_att + b_att)
        a_ij = (e_ij @ w_alpha)[:, 0]
        seg_max = jax.ops.segment_max(a_ij, recv, num_segments=N_NODES)
        seg_max = jnp.where(jnp.isfinite(seg_max), seg_max, 0.0)
        a_exp = jnp.exp(a_ij - seg_max[recv])
        denom = jax.ops.segment_sum(a_exp, recv, num_segments=N_NODES)
        alpha = a_exp / jnp.maximum(denom[recv], 1e-12)
        n_i = jax.ops.segment_sum(alpha[:, None] * wn_out, recv, num_segments=N_NODES)
        return jax.nn.elu(n_i)
    edge_index_t = jnp.stack([src, dst], axis=1)
    x = _layernorm(x + _L0_gnn_ref(x, edge_attr_128, edge_index_t, L0_gnn_W_lin, L0_gnn_b_lin, L0_gnn_W_att, L0_gnn_b_att, L0_gnn_w_alpha), axis=-1)
    return x

_drawn_inputs = setup_inputs


def setup_inputs(seed=0):
    import zlib

    import numpy as np

    out = dict(_drawn_inputs(seed))
    spreads = {'L0_gnn_b_lin': (0.0, 0.1), 'L0_gnn_b_att': (0.0, 0.8)}
    factors = {}
    for name, (base, spread) in spreads.items():
        noise = np.random.default_rng([zlib.crc32(name.encode()), seed]).standard_normal(out[name].shape)
        drawn = base * np.exp(spread * noise) if base else spread * noise
        out[name] = jnp.asarray(drawn.astype(out[name].dtype))
    for name, factor in factors.items():
        out[name] = (out[name] * factor).astype(out[name].dtype)
    return out
```

```python
from contextlib import ExitStack

import concourse.bass as bass
from concourse import mybir

F32 = mybir.dt.float32
BF16 = mybir.dt.bfloat16
I32 = mybir.dt.int32
U16 = mybir.dt.uint16
ALU = mybir.AluOpType
ACT = mybir.ActivationFunctionType
AX_X = mybir.AxisListType.X

P = 128
BIG = float(2.0 ** 100)
PAD = 255
CAP = 60.0
EPS = 1e-5
SLOPE = 0.2


def gnn_kernel(nc, x, src, dst, w_lin, b_lin, w_att, b_att, w_alpha, out):
    N, F = x.shape
    E = src.shape[0]
    NB = -(-N // P)
    TAIL = N - (NB - 1) * P
    T = -(-E // P)
    FULL = E // T
    REST = E - FULL * T
    C = 4
    CHUNK = C * P
    NCH = (P * T) // CHUNK + NB
    AHEAD = 2
    U = 6
    W = (NCH + U) * C
    R = 2 * F + 1
    HALF = 13
    PAIRS = T // (2 * HALF)
    assert F == P and PAIRS * 2 * HALF == T and NCH == 452

    SEGS = [4, 10, 24, 24]
    assert sum(SEGS) == PAIRS
    seg_cols = [2 * HALF * n for n in SEGS]
    seg_from = [sum(seg_cols[:i]) for i in range(len(SEGS))]
    SEGMAX = max(seg_cols)

    table = nc.dram_tensor("qv_table", [NB * P, 2 * F], F32, kind="Internal").ap()
    sorted_list = nc.dram_tensor("sorted_list", [P * W, 1], I32, kind="Internal").ap()
    blocks_dram = nc.dram_tensor("chunk_blocks", [1, 4 * P], I32, kind="Internal").ap()

    with ExitStack() as ctx:
        def sb(name, shape, dt):
            return ctx.enter_context(nc.sbuf_tensor(name, shape, dt))

        def psum(name, shape, dt):
            return ctx.enter_context(nc.psum_tensor(name, shape, dt))

        def sem(name):
            return ctx.enter_context(nc.semaphore(name))

        identf = sb("identf", [P, P], F32)
        identb = sb("identb", [P, P], BF16)
        big_ident = sb("big_ident", [P, P], BF16)
        before = sb("before", [P, P], F32)
        onesf = sb("onesf", [P, P], F32)
        lane_i = sb("lane_i", [P, P], I32)
        lane = sb("lane", [P, P], BF16)
        bucket_i = sb("bucket_i", [P, NB], I32)
        bucket = sb("bucket", [P, NB], F32)
        pick = sb("pick", [2 * C, C, P], BF16)
        ones_row = sb("ones_row", [1, CHUNK], BF16)
        neg_big = sb("neg_big", [1, P], BF16)
        x_sb = sb("x_sb", [P, NB, F], F32)
        w3 = sb("w3", [P, 3 * F], F32)
        bias3 = sb("bias3", [1, 3 * F], F32)
        w_row = sb("w_row", [P, F], F32)
        x_turn = sb("x_turn", [P, 2, F], F32)
        xT = sb("xT", [P, 2, P], F32)
        qv_out = sb("qv_out", [P, 2, 2 * F], F32)
        parts_mem = sb("parts_mem", [P, NB * 3 * F], BF16)
        sums = sb("sums", [P, NB, F + 1], F32)
        peak = sb("peak", [P, NB], F32)
        recv = sb("recv", [P, T], I32)
        send = sb("send", [P, T], I32)
        word = sb("word", [P, T], I32)
        block_of = sb("block_of", [P, T], BF16)
        place = sb("place", [P, T], F32)
        addr = sb("addr", [P, T], I32)
        match = sb("match", [P, SEGMAX], BF16)
        count = sb("count", [P, SEGMAX], F32)
        totals = sb("totals", [P, NB], F32)
        run = sb("run", [P, NB], F32)
        nb_f = sb("nb_f", [P, NB], F32)
        nb_i = sb("nb_i", [P, NB], I32)
        ends = sb("ends", [P, NB], F32)
        chunk_i = sb("chunk_i", [P, 4], I32)
        chunk_no = sb("chunk_no", [P, 4], F32)
        passed = sb("passed", [P, 4, NB], F32)
        blk_f = sb("blk_f", [P, 4], F32)
        blk_i = sb("blk_i", [P, 4], I32)
        staged = sb("staged", [P, 2, 2, HALF], I32)
        words = sb("words", [P, W], I32)
        senders = sb("senders", [P, W], I32)
        lanes = sb("lanes", [P, W], BF16)
        blocks = sb("blocks", [1, 4 * P], I32)
        index = sb("index", [P, U, C], I32)
        rows = sb("rows", [P, U, C, R], F32)
        onehot = sb("onehot", [P, U, C, P], BF16)
        onehotT = sb("onehotT", [P, 3, CHUNK], BF16)
        leaky = sb("leaky", [P, CHUNK], F32)
        sloped = sb("sloped", [P, 2, CHUNK], F32)
        waste = sb("waste", [P, C, F], F32)
        logit = sb("logit", [P, 2, C], F32)
        logit_parts = sb("logit_parts", [P, 2, 2 * C], BF16)
        logitT = sb("logitT", [2 * C, 2, P], BF16)
        chunk_max = sb("chunk_max", [P, 1], F32)
        new_max = sb("new_max", [P, 1], F32)
        peak_hi = sb("peak_hi", [P, 3], BF16)
        peak_lo = sb("peak_lo", [P, 3], BF16)
        rounded = sb("rounded", [P, 1], F32)
        growth = sb("growth", [P, 2], F32)
        shrink = sb("shrink", [P, 2], F32)
        below = sb("below", [P, C], F32)
        capped = sb("capped", [P, 2, C], F32)
        weight = sb("weight", [P, 2, C], F32)
        weighted = sb("weighted", [P, 2, C, P], F32)
        recip = sb("recip", [P, NB], F32)
        stats = sb("stats", [P, NB, 6], F32)
        moments = sb("moments", [P, NB, 2], F32)

        onehotT_ps = psum("onehotT_ps", [P, 2, 2 * CHUNK], BF16)
        hidden_ps = psum("hidden_ps", [P, 2, CHUNK], F32)
        masked_ps = psum("masked_ps", [P, CHUNK], F32)
        sums_ps = psum("sums_ps", [P, CHUNK], F32)
        logitT_ps = psum("logitT_ps", [2 * C, 2 * CHUNK], BF16)
        peak_ps = psum("peak_ps", [P, 4, P], F32)
        turn_ps = (masked_ps, sums_ps)

        p_parts = parts_mem[:].rearrange("p (b s f) -> p b s f", s=3, f=F)
        elu_work = parts_mem[:].bitcast(F32)[:, 0:NB * F].rearrange("p (b f) -> p b f", f=F)
        p_f32 = sums[:, :, 0:F]

        filled = sem("filled")
        consts = sem("consts")
        consts_v = sem("consts_v")
        edges_in = sem("edges_in")
        x_in = sem("x_in")
        weights_in = sem("weights_in")
        prepared = sem("prepared")
        counted = sem("counted")
        totals_ps = sem("totals_ps")
        based = sem("based")
        ranked = sem("ranked")
        addressed = sem("addressed")
        seg_ready = sem("seg_ready")
        padded = sem("padded")
        scatter_staged = sem("scatter_staged")
        scattered = [sem("scattered0"), sem("scattered1")]
        blk_ready = sem("blk_ready")
        blk_stored = sem("blk_stored")
        blk_loaded = sem("blk_loaded")
        x_staged = sem("x_staged")
        xT_ps = sem("xT_ps")
        xT_ready = sem("xT_ready")
        pqv_ps = sem("pqv_ps")
        p_ready = sem("p_ready")
        qv_ready = sem("qv_ready")
        qv_stored = [sem("qv_stored0"), sem("qv_stored1")]
        words_in = sem("words_in")
        unpacked = sem("unpacked")
        split = sem("split")
        indexed = sem("indexed")
        gathered = [sem(f"gathered{r}") for r in range(U)]
        onehot_ready = sem("onehot_ready")
        onehotT_done = sem("onehotT_done")
        onehotT_ready = sem("onehotT_ready")
        hidden_done = sem("hidden_done")
        sloped_ready = sem("sloped_ready")
        leaky_ready = sem("leaky_ready")
        logit_ready = sem("logit_ready")
        logit_hi_ready = sem("logit_hi_ready")
        logit_lo_ready = sem("logit_lo_ready")
        logitT_done = sem("logitT_done")
        logitT_ready = sem("logitT_ready")
        masked_done = sem("masked_done")
        chunk_max_ready = sem("chunk_max_ready")
        new_max_ready = sem("new_max_ready")
        peak_hi_ready = sem("peak_hi_ready")
        peak_lo_ready = sem("peak_lo_ready")
        rounded_ready = sem("rounded_ready")
        growth_ready = sem("growth_ready")
        peak_ready = sem("peak_ready")
        edge_peak_done = sem("edge_peak_done")
        below_ready = sem("below_ready")
        capped_ready = sem("capped_ready")
        weight_ready = sem("weight_ready")
        shrink_ready = sem("shrink_ready")
        weighted_ready = sem("weighted_ready")
        chunk_sums_done = sem("chunk_sums_done")
        sums_ready = sem("sums_ready")
        finish = sem("finish")
        exp_done = sem("exp_done")
        sqrt_done = sem("sqrt_done")
        normed = sem("normed")
        stored = sem("stored")

        BODIES = NCH // U
        PAIRS_X = NB // 2
        assert NB % 2 == 1

        def chunks(eng, step):
            for j in range(U):
                step(0, j)
            with eng.Fori(1, BODIES) as i:
                for j in range(U):
                    step(i, j)
            for j in range(NCH - BODIES * U):
                step(BODIES, j)

        def past(k, n):
            return not isinstance(k, int) or k >= n

        block = ctx.enter_context(nc.Block())

        @block.sync
        def _(sp):
            sp.wait_ge(filled, 4)
            for t, a in ((recv, src), (send, dst)):
                sp.dma_start(t[0:FULL, :], a[0:FULL * T].rearrange("(p c) -> p c", c=T)).then_inc(edges_in, 16)
                sp.dma_start(t[FULL:FULL + 1, 0:REST],
                             a[FULL * T:E].rearrange("(p c) -> p c", p=1)).then_inc(edges_in, 16)
            sp.dma_start(w3[:, 0:F], w_att[0:F, :]).then_inc(weights_in, 16)
            sp.dma_start(w3[:, F:2 * F], w_att[F:2 * F, :]).then_inc(weights_in, 16)
            sp.dma_start(w3[:, 2 * F:3 * F], w_lin).then_inc(weights_in, 16)
            sp.dma_start(bias3[0:1, 0:F], b_att.rearrange("(a d) -> a d", a=1)).then_inc(weights_in, 16)
            sp.dma_start(bias3[0:1, 2 * F:3 * F], b_lin.rearrange("(a d) -> a d", a=1)).then_inc(weights_in, 16)
            sp.dma_start(w_row[:], w_alpha.rearrange("d a -> a d").to_broadcast([P, F])).then_inc(weights_in, 16)
            sp.dma_start(x_sb[:, 0:NB - 1, :],
                         x[0:(NB - 1) * P, :].rearrange("(b p) f -> p b f", p=P)).then_inc(x_in, 16)
            sp.dma_start(x_sb[0:TAIL, NB - 1, :], x[(NB - 1) * P:N, :]).then_inc(x_in, 16)
            sp.wait_ge(filled, 5)
            sp.dma_start(sorted_list.rearrange("(p w) a -> p (w a)", w=W), words[:]).then_inc(padded, 16)
            def store_rows(b, j):
                sp.wait_ge(qv_ready, b + 1)
                sp.dma_start(table[bass.ds(b * P, P), :], qv_out[:, j, :]).then_inc(qv_stored[j], 16)

            with sp.Fori(0, PAIRS_X) as i:
                for j in (0, 1):
                    store_rows(i * 2 + j, j)
            store_rows(NB - 1, 0)
            sp.wait_ge(blk_ready, 1)
            sp.dma_start(blocks_dram.rearrange("a (p g) -> (a p) g", g=4), blk_i[:]).then_inc(blk_stored, 16)
            sp.wait_ge(blk_stored, 16)
            sp.dma_start(blocks[:], blocks_dram).then_inc(blk_loaded, 16)
            sp.wait_ge(scattered[0], 16 * HALF * PAIRS)
            sp.wait_ge(scattered[1], 16 * HALF * PAIRS)
            sp.dma_start(words[:], sorted_list.rearrange("(p w) a -> p (w a)", w=W)).then_inc(words_in, 16)
            sp.wait_ge(normed, NB)
            sp.dma_start(out[0:(NB - 1) * P, :].rearrange("(b p) f -> p b f", p=P),
                         x_sb[:, 0:NB - 1, :]).then_inc(stored, 16)
            sp.dma_start(out[(NB - 1) * P:N, :], x_sb[0:TAIL, NB - 1, :]).then_inc(stored, 16)
            sp.wait_ge(qv_stored[0], 16 * (PAIRS_X + 1))
            sp.wait_ge(qv_stored[1], 16 * PAIRS_X)
            sp.wait_ge(stored, 32)

        @block.gpsimd
        def _(pool):
            g = nc.gpsimd
            g.iota(lane_i[:], pattern=[[1, P]], base=0, channel_multiplier=0).then_inc(consts, 1)
            g.iota(bucket_i[:], pattern=[[1, NB]], base=0, channel_multiplier=0).then_inc(consts, 1)
            g.iota(chunk_i[:], pattern=[[1, 4]], base=0, channel_multiplier=4).then_inc(consts, 1)
            pool.wait_ge(filled, 10)
            for t, one in ((identf, 1.0), (identb, 1.0), (big_ident, BIG)):
                g.affine_select(out=t[:], in_=t[:], compare_op=ALU.not_equal, fill=one, base=0,
                                pattern=[[-1, P]], channel_multiplier=1).then_inc(consts, 1)
            g.affine_select(out=before[:], in_=before[:], compare_op=ALU.is_gt, fill=0.0, base=0,
                            pattern=[[1, P]], channel_multiplier=-1).then_inc(consts, 1)
            g.affine_select(out=pick[:], in_=pick[:], compare_op=ALU.not_equal, fill=1.0, base=0,
                            pattern=[[-1, C], [0, P]], channel_multiplier=1).then_inc(consts, 1)
            pool.wait_ge(consts, 8)
            g.affine_select(out=pick[:], in_=pick[:], compare_op=ALU.not_equal, fill=1.0, base=-C,
                            pattern=[[-1, C], [0, P]], channel_multiplier=1).then_inc(consts, 1)

            pool.wait_ge(padded, 16)
            with pool.Fori(0, PAIRS) as i:
                for h in (0, 1):
                    pool.wait_ge(scatter_staged, i * 2 + h + 1)
                    pool.nop(nofuse=True)
                    for c in range(HALF):
                        g.indirect_dma_start(
                            out=sorted_list, in_=staged[:, h, 1, c:c + 1], in_offset=None,
                            out_offset=bass.IndirectOffsetOnAxis(ap=staged[:, h, 0, c:c + 1], axis=0),
                        ).then_inc(scattered[h], 16)

            pool.wait_ge(qv_stored[0], 16 * (PAIRS_X + 1))
            pool.wait_ge(qv_stored[1], 16 * PAIRS_X)

            def gather(i, j):
                k = i * U + j
                pool.wait_ge(indexed, k + 1)
                if past(k, U):
                    pool.wait_ge(chunk_sums_done, k - U + 1)
                pool.nop(nofuse=True)
                for c in range(C):
                    g.indirect_dma_start(
                        out=rows[:, j, c, 0:2 * F], out_offset=None, in_=table,
                        in_offset=bass.IndirectOffsetOnAxis(ap=index[:, j, c:c + 1], axis=0),
                    ).then_inc(gathered[j], 16)

            chunks(pool, gather)
            for k in range(NCH, NCH + AHEAD):
                gather(k // U, k % U)

        @block.scalar
        def _(act):
            a = nc.scalar

            act.wait_ge(x_in, 32)

            def stage_x(b, j):
                if past(b, 2):
                    act.wait_ge(xT_ps, b - 1)
                a.activation(x_turn[:, j, :], x_sb[:, bass.ds(b, 1), :].rearrange("p a f -> p (a f)"),
                             ACT.Copy).then_inc(x_staged, 1)

            def copy_xT(b, j):
                act.wait_ge(xT_ps, b + 1)
                a.activation(xT[:, j, :], turn_ps[j][:, 0:P], ACT.Copy).then_inc(xT_ready, 1)

            def copy_pqv(i, j):
                b = i * 2 + j
                act.wait_ge(pqv_ps, b + 1)
                a.activation(p_f32[:, bass.ds(b, 1), :].rearrange("p a f -> p (a f)"),
                             hidden_ps[:, j, 0:F], ACT.Copy).then_inc(p_ready, 1)
                if past(b, 2):
                    act.wait_ge(qv_stored[j], i * 16)
                a.activation(qv_out[:, j, :], hidden_ps[:, j, F:3 * F], ACT.Copy).then_inc(qv_ready, 1)

            def copy_pair(i):
                for j in (0, 1):
                    stage_x(i * 2 + j, j)
                for j in (0, 1):
                    copy_xT(i * 2 + j, j)
                for j in (0, 1):
                    copy_pqv(i, j)

            copy_pair(0)
            with act.Fori(1, PAIRS_X) as i:
                copy_pair(i)
            stage_x(NB - 1, 0)
            copy_xT(NB - 1, 0)
            copy_pqv(PAIRS_X, 0)

            def stage(i, h):
                if past(i, 1):
                    act.wait_ge(scattered[h], i * (16 * HALF))
                at = (i * 2 + h) * HALF
                a.activation(staged[:, h, 0, :], addr[:, bass.ds(at, HALF)], ACT.Copy)
                a.activation(staged[:, h, 1, :], word[:, bass.ds(at, HALF)], ACT.Copy).then_inc(scatter_staged, 1)

            done = 0
            for s, n in enumerate(SEGS):
                act.wait_ge(seg_ready, s + 1)
                if s == 0:
                    for h in (0, 1):
                        stage(0, h)
                with act.Fori(max(done, 1), done + n) as i:
                    for h in (0, 1):
                        stage(i, h)
                done += n

            def stage_index(k, r, rounds):
                if past(k, U):
                    act.wait_ge(gathered[r], rounds * (16 * C))
                a.activation(index[:, r, :], senders[:, bass.ds(k * C, C)], ACT.Copy).then_inc(indexed, 1)

            def copy_onehotT(k, j):
                act.wait_ge(onehotT_done, k + 1)
                if past(k, 3):
                    act.wait_ge(edge_peak_done, k - 2)
                a.activation(onehotT[:, j % 3, :], onehotT_ps[:, j % 2, 0:CHUNK], ACT.Copy).then_inc(onehotT_ready, 1)

            def slope(k, j):
                act.wait_ge(hidden_done, k + 1)
                if past(k, 2):
                    act.wait_ge(leaky_ready, k - 1)
                a.activation(sloped[:, j % 2, :], hidden_ps[:, j % 2, :], ACT.Copy, scale=SLOPE).then_inc(sloped_ready, 1)

            def copy_logitT(k, j):
                act.wait_ge(logitT_done, k + 1)
                if past(k, 2):
                    act.wait_ge(masked_done, k - 1)
                a.activation(logitT[:, j % 2, :], logitT_ps[:, 0:P], ACT.Copy).then_inc(logitT_ready, 1)

            def exponentials(k, j):
                act.wait_ge(growth_ready, k + 1)
                if past(k, 2):
                    act.wait_ge(sums_ready, k - 1)
                a.activation(shrink[:, j % 2:j % 2 + 1], growth[:, j % 2:j % 2 + 1], ACT.Exp).then_inc(shrink_ready, 1)
                act.wait_ge(capped_ready, k + 1)
                if past(k, 2):
                    act.wait_ge(weighted_ready, k - 1)
                a.activation(weight[:, j % 2, :], capped[:, j % 2, :], ACT.Exp).then_inc(weight_ready, 1)

            act.wait_ge(unpacked, 3)
            for k in range(U - 1):
                stage_index(k, k, 0)
            copy_onehotT(0, 0)
            copy_onehotT(1, 1)
            slope(0, 0)
            slope(1, 1)
            copy_logitT(0, 0)

            def step(i, j):
                k = i * U + j
                exponentials(k, j)
                copy_onehotT(k + 2, j + 2)
                slope(k + 2, j + 2)
                copy_logitT(k + 1, j + 1)
                stage_index(k + U - 1, (j + U - 1) % U, i + (j >= 1))

            chunks(act, step)

            act.wait_ge(finish, 4)
            a.activation(elu_work, elu_work, ACT.Exp).then_inc(exp_done, 1)
            act.wait_ge(finish, 9)
            a.activation(recip[:], recip[:], ACT.Sqrt).then_inc(sqrt_done, 1)

        @block.tensor
        def _(pe):
            t = nc.tensor
            pe.wait_ge(consts, 9)
            pe.wait_ge(filled, 15)
            pe.wait_ge(counted, NB + 1)
            t.matmul(peak_ps[:, 0, 0:NB], before[:], totals[:], start=True, stop=True)
            t.matmul(peak_ps[:, 1, 0:NB], onesf[:], totals[:], start=True, stop=True).then_inc(totals_ps, 1)

            pe.wait_ge(weights_in, 6 * 16)

            def turn_x(b, j):
                if past(b, 2):
                    pe.wait_ge(xT_ready, b - 1)
                pe.wait_ge(x_staged, b + 1)
                t.transpose(turn_ps[j][:, 0:P], x_turn[:, j, :], identf[:]).then_inc(xT_ps, 1)

            def project(b, j):
                pe.wait_ge(xT_ready, b + 1)
                if past(b, 2):
                    pe.wait_ge(qv_ready, b - 1)
                t.matmul(hidden_ps[:, j, 0:3 * F], xT[:, j, :], w3[:], start=True, stop=False)
                t.matmul(hidden_ps[:, j, 0:3 * F], onesf[0:1, :], bias3[:], start=False, stop=True).then_inc(pqv_ps, 1)

            def pair(i):
                for j in (0, 1):
                    turn_x(i * 2 + j, j)
                for j in (0, 1):
                    project(i * 2 + j, j)

            pair(0)
            with pe.Fori(1, PAIRS_X) as i:
                pair(i)
            turn_x(NB - 1, 0)
            project(NB - 1, 0)

            def turn_onehot(k, j):
                pe.wait_ge(onehot_ready, k + 1)
                if past(k, 2):
                    pe.wait_ge(onehotT_ready, k - 1)
                for c in range(C):
                    mm = t.transpose(onehotT_ps[:, j % 2, c * P:(c + 1) * P], onehot[:, j % U, c, :], identb[:])
                mm.then_inc(onehotT_done, 1)

            def turn_logit(k, j):
                pe.wait_ge(logit_lo_ready, k + 1)
                if past(k, 1):
                    pe.wait_ge(logitT_ready, k)
                t.transpose(logitT_ps[:, 0:P], logit_parts[:, j % 2, :], identb[:]).then_inc(logitT_done, 1)

            def hidden(k, j, rounds):
                b = pe.value_load(blocks[0:1, bass.ds(k, 1)], min_val=0, max_val=NB - 1)
                pe.wait_ge(onehotT_ready, k + 1)
                pe.wait_ge(gathered[j % U], rounds * (16 * C))
                if past(k, 2):
                    pe.wait_ge(leaky_ready, k - 1)
                for c in range(C):
                    here = hidden_ps[:, j % 2, c * P:(c + 1) * P]
                    for s in range(3):
                        t.matmul(here, onehotT[:, j % 3, c * P:(c + 1) * P],
                                 p_parts[:, bass.ds(b, 1), s, :].rearrange("p a f -> p (a f)"),
                                 start=(s == 0), stop=False)
                    mm = t.matmul(here, identf[:], rows[:, j % U, c, 0:F], start=False, stop=True)
                mm.then_inc(hidden_done, 1)

            def mask(k, j):
                pe.wait_ge(logitT_ready, k + 1)
                if past(k, 1):
                    pe.wait_ge(chunk_max_ready, k)
                whole = masked_ps[:]
                t.matmul(whole, neg_big[:], ones_row[:], start=True, stop=False, skip_group_check=True)
                t.matmul(whole, big_ident[:], onehotT[:, j % 3, :], start=False, stop=False, skip_group_check=True)
                for c in range(C):
                    mm = t.matmul(whole[:, c * P:(c + 1) * P], pick[:, c, :], logitT[:, j % 2, :],
                                  start=False, stop=(c == C - 1), skip_group_check=True)
                mm.then_inc(masked_done, 1)

            def edge_peak(k, j):
                pe.wait_ge(peak_lo_ready, k + 1)
                if past(k, 1):
                    pe.wait_ge(below_ready, k)
                for c in range(C):
                    here = peak_ps[:, 0, c:c + 1]
                    lhs = onehotT[:, j % 3, c * P:(c + 1) * P]
                    t.matmul(here, lhs, peak_hi[:, j % 3:j % 3 + 1], start=True, stop=False)
                    mm = t.matmul(here, lhs, peak_lo[:, j % 3:j % 3 + 1], start=False, stop=True)
                mm.then_inc(edge_peak_done, 1)

            def chunk_sums(k, j):
                pe.wait_ge(weighted_ready, k + 1)
                if past(k, 1):
                    pe.wait_ge(sums_ready, k)
                for c in range(C):
                    mm = t.matmul(sums_ps[:, 0:F + 1], weighted[:, j % 2, c, :], rows[:, j % U, c, F:R],
                                  start=(c == 0), stop=(c == C - 1))
                mm.then_inc(chunk_sums_done, 1)

            pe.wait_ge(blk_loaded, 16)
            pe.wait_ge(split, 6)
            for k in (0, 1):
                turn_onehot(k, k)
            for k in (0, 1):
                hidden(k, k, 1)
            turn_logit(0, 0)
            mask(0, 0)
            edge_peak(0, 0)

            def step(i, j):
                k = i * U + j
                turn_onehot(k + 2, j + 2)
                turn_logit(k + 1, j + 1)
                hidden(k + 2, j + 2, i + 1 + (j + 2) // U)
                mask(k + 1, j + 1)
                chunk_sums(k, j)
                edge_peak(k + 1, j + 1)

            chunks(pe, step)

        @block.vector
        def _(dve):
            v = nc.vector
            v.memset(recv[:, REST:], NB * P - 1).then_inc(filled, 1)
            v.memset(send[:, REST:], 0).then_inc(filled, 1)
            v.memset(x_sb[:, NB - 1, :], 0.0).then_inc(filled, 1)
            v.memset(bias3[:], 0.0).then_inc(filled, 1)
            v.memset(words[:], PAD).then_inc(filled, 1)
            v.memset(identf[:], 0.0).then_inc(filled, 1)
            v.memset(identb[:], 0.0).then_inc(filled, 1)
            v.memset(big_ident[:], 0.0).then_inc(filled, 1)
            v.memset(before[:], 1.0).then_inc(filled, 1)
            v.memset(pick[:], 0.0).then_inc(filled, 1)
            v.memset(onesf[:], 1.0).then_inc(filled, 1)
            v.memset(ones_row[:], 1.0).then_inc(filled, 1)
            v.memset(neg_big[:], -BIG).then_inc(filled, 1)
            v.memset(peak[:], -BIG).then_inc(filled, 1)
            v.memset(rows[:, :, :, 2 * F:R], 1.0).then_inc(filled, 1)
            dve.wait_ge(consts, 3)
            v.tensor_copy(lane[:], lane_i[:]).then_inc(consts_v, 1)
            v.tensor_copy(bucket[:], bucket_i[:]).then_inc(consts_v, 1)
            v.tensor_copy(chunk_no[:], chunk_i[:]).then_inc(consts_v, 1)

            dve.wait_ge(edges_in, 64)
            v.tensor_scalar(addr[:], recv[:], 7, None, ALU.arith_shift_right).then_inc(prepared, 1)
            dve.wait_ge(prepared, 1)
            v.tensor_scalar(recv[:], recv[:], P - 1, None, ALU.bitwise_and).then_inc(prepared, 1)
            v.tensor_copy(block_of[:], addr[:]).then_inc(prepared, 1)
            dve.wait_ge(prepared, 3)
            v.scalar_tensor_tensor(out=word[:], in0=send[:], scalar=256.0, in1=recv[:],
                                   op0=ALU.mult, op1=ALU.add).then_inc(prepared, 1)
            dve.wait_ge(consts_v, 3)
            dve.wait_ge(prepared, 4)
            v.memset(place[:], 0.0).then_inc(counted, 1)

            with dve.Fori(0, NB) as b:
                dve.wait_ge(counted, b + 1)
                v.tensor_scalar(place[:], block_of[:], bucket[:, bass.ds(b, 1)], None, ALU.is_equal,
                                ALU.add, accum_out=totals[:, bass.ds(b, 1)]).then_inc(counted, 1)

            dve.wait_ge(totals_ps, 1)
            v.tensor_scalar(nb_i[:], peak_ps[:, 1, 0:NB], float(CHUNK - 1), None, ALU.add).then_inc(based, 1)
            dve.wait_ge(based, 1)
            v.tensor_scalar(nb_i[:], nb_i[:], CHUNK.bit_length() - 1, None, ALU.arith_shift_right).then_inc(based, 1)
            dve.wait_ge(based, 2)
            v.tensor_copy(nb_f[:], nb_i[:]).then_inc(based, 1)
            dve.wait_ge(based, 3)
            v.tensor_tensor_scan(ends[:], nb_f[:], nb_f[:], 0.0, ALU.add, ALU.max).then_inc(based, 1)
            dve.wait_ge(based, 4)
            v.tensor_tensor(run[:], ends[:], nb_f[:], ALU.subtract).then_inc(based, 1)
            dve.wait_ge(based, 5)
            v.scalar_tensor_tensor(out=run[:], in0=run[:], scalar=float(CHUNK), in1=peak_ps[:, 0, 0:NB],
                                   op0=ALU.mult, op1=ALU.add).then_inc(based, 1)
            v.tensor_tensor(passed[:], ends[:].unsqueeze(1).to_broadcast([P, 4, NB]),
                            chunk_no[:].unsqueeze(2).to_broadcast([P, 4, NB]), ALU.is_le).then_inc(based, 1)
            dve.wait_ge(based, 7)
            v.tensor_reduce(blk_f[:], passed[:], AX_X, ALU.add).then_inc(based, 1)
            dve.wait_ge(based, 8)
            v.tensor_scalar(blk_i[:], blk_f[:], float(NB - 1), None, ALU.min).then_inc(blk_ready, 1)
            dve.wait_ge(blk_ready, 1)
            v.memset(place[:], 0.0).then_inc(ranked, 1)

            for s, (at, n) in enumerate(zip(seg_from, seg_cols)):
                with dve.Fori(0, NB) as b:
                    base = (b + s * NB) * 4 + 1
                    dve.wait_ge(ranked, base)
                    v.tensor_scalar(match[:, 0:n], block_of[:, at:at + n], bucket[:, bass.ds(b, 1)], None,
                                    ALU.is_equal).then_inc(ranked, 1)
                    dve.wait_ge(ranked, base + 1)
                    v.tensor_tensor_scan(count[:, 0:n], match[:, 0:n], match[:, 0:n], run[:, bass.ds(b, 1)],
                                         ALU.add, ALU.max).then_inc(ranked, 1)
                    dve.wait_ge(ranked, base + 2)
                    dve.nop(nofuse=True)
                    v.copy_predicated(place[:, at:at + n], match[:, 0:n].bitcast(U16), count[:, 0:n]).then_inc(ranked, 1)
                    v.tensor_copy(run[:, bass.ds(b, 1)], count[:, n - 1:n]).then_inc(ranked, 1)
                dve.wait_ge(ranked, (s + 1) * NB * 4 + 1)
                cols = slice(at, at + n)
                v.tensor_scalar(recv[:, cols], place[:, cols], -1.0, None, ALU.add).then_inc(addressed, 1)
                dve.wait_ge(addressed, 3 * s + 1)
                v.tensor_scalar(send[:, cols], recv[:, cols], P - 1, None, ALU.bitwise_and).then_inc(addressed, 1)
                dve.wait_ge(addressed, 3 * s + 2)
                v.tensor_scalar(recv[:, cols], recv[:, cols], 7, None, ALU.arith_shift_right).then_inc(addressed, 1)
                dve.wait_ge(addressed, 3 * s + 3)
                v.scalar_tensor_tensor(out=addr[:, cols], in0=send[:, cols], scalar=float(W), in1=recv[:, cols],
                                       op0=ALU.mult, op1=ALU.add).then_inc(seg_ready, 1)

            dve.wait_ge(p_ready, NB)
            for s in range(3):
                v.tensor_copy(p_parts[:, :, s, :], p_f32).then_inc(split, 1)
                dve.wait_ge(split, 2 * s + 1)
                if s < 2:
                    v.tensor_tensor(p_f32, p_f32, p_parts[:, :, s, :], ALU.subtract).then_inc(split, 1)
                    dve.wait_ge(split, 2 * s + 2)
            v.memset(sums[:], 0.0).then_inc(split, 1)

            dve.wait_ge(words_in, 16)
            v.tensor_scalar(senders[:], words[:], 8, None, ALU.arith_shift_right).then_inc(unpacked, 1)
            dve.wait_ge(unpacked, 1)
            v.tensor_scalar(words[:], words[:], 255, None, ALU.bitwise_and).then_inc(unpacked, 1)
            dve.wait_ge(unpacked, 2)
            v.tensor_copy(lanes[:], words[:]).then_inc(unpacked, 1)
            dve.wait_ge(unpacked, 3)
            dve.wait_ge(weights_in, 6 * 16)
            dve.wait_ge(blk_loaded, 16)

            def make_onehot(k, j):
                v.tensor_tensor(onehot[:, j % U], lane[:].unsqueeze(1).to_broadcast([P, C, P]),
                                lanes[:, bass.ds(k * C, C)].unsqueeze(2).to_broadcast([P, C, P]),
                                ALU.is_equal).then_inc(onehot_ready, 1)

            def logits(k, j):
                if past(k, 1):
                    dve.wait_ge(logit_ready, k)
                dve.wait_ge(sloped_ready, k + 1)
                v.tensor_tensor(leaky[:], hidden_ps[:, j % 2, :], sloped[:, j % 2, :], ALU.max).then_inc(leaky_ready, 1)
                dve.wait_ge(leaky_ready, k + 1)
                for c in range(C):
                    dot = v.tensor_tensor_reduce(waste[:, c, :], leaky[:, c * P:(c + 1) * P], w_row[:], 1.0, 0.0,
                                                 ALU.mult, ALU.add, logit[:, j % 2, c:c + 1])
                dot.then_inc(logit_ready, 1)

            def split_logits(k, j):
                dve.wait_ge(logit_ready, k + 1)
                if past(k, 2):
                    dve.wait_ge(logitT_done, k - 1)
                parts = logit_parts[:, j % 2, :]
                v.tensor_copy(parts[:, 0:C], logit[:, j % 2, :]).then_inc(logit_hi_ready, 1)
                dve.wait_ge(logit_hi_ready, k + 1)
                v.tensor_tensor(parts[:, C:2 * C], logit[:, j % 2, :], parts[:, 0:C],
                                ALU.subtract).then_inc(logit_lo_ready, 1)

            def raise_peak(k, j, b):
                dve.wait_ge(masked_done, k + 1)
                v.tensor_reduce(chunk_max[:], masked_ps[:], AX_X, ALU.max).then_inc(chunk_max_ready, 1)
                dve.wait_ge(chunk_max_ready, k + 1)
                if past(k, 1):
                    dve.wait_ge(peak_ready, k)
                at = peak[:, bass.ds(b, 1)]
                v.tensor_tensor(new_max[:], chunk_max[:], at, ALU.max).then_inc(new_max_ready, 1)
                hi, lo = peak_hi[:, j % 3:j % 3 + 1], peak_lo[:, j % 3:j % 3 + 1]
                dve.wait_ge(new_max_ready, k + 1)
                v.tensor_copy(hi, new_max[:]).then_inc(peak_hi_ready, 1)
                dve.wait_ge(peak_hi_ready, k + 1)
                v.tensor_tensor(lo, new_max[:], hi, ALU.subtract).then_inc(peak_lo_ready, 1)
                dve.wait_ge(peak_lo_ready, k + 1)
                v.tensor_tensor(rounded[:], hi, lo, ALU.add).then_inc(rounded_ready, 1)
                dve.wait_ge(rounded_ready, k + 1)
                if past(k, 2):
                    dve.wait_ge(shrink_ready, k - 1)
                v.tensor_tensor(growth[:, j % 2:j % 2 + 1], at, rounded[:], ALU.subtract).then_inc(growth_ready, 1)
                dve.wait_ge(growth_ready, k + 1)
                v.tensor_tensor(at, hi, lo, ALU.add).then_inc(peak_ready, 1)

            def exponent(k, j):
                dve.wait_ge(edge_peak_done, k + 1)
                v.tensor_tensor(below[:], logit[:, j % 2, :], peak_ps[:, 0, 0:C], ALU.subtract).then_inc(below_ready, 1)
                dve.wait_ge(below_ready, k + 1)
                if past(k, 2):
                    dve.wait_ge(weight_ready, k - 1)
                v.tensor_scalar(capped[:, j % 2, :], below[:], CAP, None, ALU.min).then_inc(capped_ready, 1)

            def weigh(k, j):
                dve.wait_ge(weight_ready, k + 1)
                if past(k, 2):
                    dve.wait_ge(chunk_sums_done, k - 1)
                v.tensor_tensor(weighted[:, j % 2], onehot[:, j % U],
                                weight[:, j % 2, :].unsqueeze(2).to_broadcast([P, C, P]),
                                ALU.mult).then_inc(weighted_ready, 1)

            def add_sums(k, j, b):
                dve.wait_ge(chunk_sums_done, k + 1)
                dve.wait_ge(shrink_ready, k + 1)
                if past(k, 1):
                    dve.wait_ge(sums_ready, k)
                at = sums[:, bass.ds(b, 1), :].rearrange("p a f -> p (a f)")
                v.scalar_tensor_tensor(out=at, in0=at, scalar=shrink[:, j % 2:j % 2 + 1], in1=sums_ps[:, 0:F + 1],
                                       op0=ALU.mult, op1=ALU.add).then_inc(sums_ready, 1)

            def block_at(k):
                return dve.value_load(blocks[0:1, bass.ds(k, 1)], min_val=0, max_val=NB - 1)

            for k in range(3):
                make_onehot(k, k)
            logits(0, 0)
            split_logits(0, 0)
            raise_peak(0, 0, block_at(0))

            def step(i, j):
                k = i * U + j
                b, following = block_at(k), block_at(k + 1)
                exponent(k, j)
                logits(k + 1, j + 1)
                split_logits(k + 1, j + 1)
                weigh(k, j)
                make_onehot(k + 3, j + 3)
                raise_peak(k + 1, j + 1, following)
                add_sums(k, j, b)

            chunks(dve, step)

            dve.wait_ge(sums_ready, NCH)
            v.tensor_scalar(recip[:], sums[:, :, F], 1e-12, None, ALU.max).then_inc(finish, 1)
            dve.wait_ge(finish, 1)
            v.reciprocal(recip[:], recip[:]).then_inc(finish, 1)
            dve.wait_ge(finish, 2)
            n = sums[:, :, 0:F]
            v.tensor_tensor(n, n, recip[:].unsqueeze(2).to_broadcast([P, NB, F]), ALU.mult).then_inc(finish, 1)
            dve.wait_ge(finish, 3)
            v.tensor_scalar(elu_work, n, 0.0, None, ALU.min).then_inc(finish, 1)
            v.scalar_tensor_tensor(out=x_sb[:], in0=n, scalar=0.0, in1=x_sb[:], op0=ALU.max, op1=ALU.add).then_inc(finish, 1)
            dve.wait_ge(finish, 5)
            dve.wait_ge(exp_done, 1)
            v.scalar_tensor_tensor(out=x_sb[:], in0=elu_work, scalar=-1.0, in1=x_sb[:], op0=ALU.add, op1=ALU.add).then_inc(finish, 1)
            dve.wait_ge(finish, 6)
            for b in range(NB):
                last = v.bn_stats(stats[:, b, :], x_sb[:, b, :])
            last.then_inc(finish, 1)
            dve.wait_ge(finish, 7)
            for b in range(NB):
                last = v.bn_aggr(moments[:, b, :], stats[:, b, :])
            last.then_inc(finish, 1)
            dve.wait_ge(finish, 8)
            v.tensor_scalar(recip[:], moments[:, :, 1], EPS, None, ALU.add).then_inc(finish, 1)
            dve.wait_ge(sqrt_done, 1)
            v.reciprocal(recip[:], recip[:]).then_inc(finish, 1)
            dve.wait_ge(finish, 10)
            for b in range(NB):
                v.tensor_scalar(x_sb[:, b, :], x_sb[:, b, :], moments[:, b, 0:1], recip[:, b:b + 1],
                                ALU.subtract, ALU.mult).then_inc(normed, 1)


_INS = ["x", "src", "dst", "L0_gnn_W_lin", "L0_gnn_b_lin", "L0_gnn_W_att", "L0_gnn_b_att", "L0_gnn_w_alpha"]


def kernel(**inputs):
    import numpy as _np
    import concourse.bacc as _bacc
    from concourse import mybir as _mybir
    from concourse.bass_utils import run_bass_kernel_spmd as _run

    nc = _bacc.Bacc("TRN2", target_bir_lowering=False, num_devices=1)
    arrays, args = {}, []
    for name in _INS:
        a = _np.ascontiguousarray(inputs[name])
        arrays[f"in_{name}"] = a
        args.append(nc.dram_tensor(f"in_{name}", a.shape, _mybir.dt.from_np(a.dtype), kind="ExternalInput").ap())
    shape = inputs["x"].shape
    args.append(nc.dram_tensor("out_0", shape, F32, kind="ExternalOutput").ap())
    gnn_kernel(nc, *args)
    r = _run(nc, [arrays], core_ids=[0])
    return r.results[0]["out_0"]
```

```python
from contextlib import ExitStack

import concourse.bass as bass
from concourse import mybir

F32 = mybir.dt.float32
BF16 = mybir.dt.bfloat16
I32 = mybir.dt.int32
U16 = mybir.dt.uint16
ALU = mybir.AluOpType
ACT = mybir.ActivationFunctionType
AX_X = mybir.AxisListType.X

P = 128
BIG = float(2.0 ** 100)
LOW = float(2.0 ** 90)
EPS = 1e-5
SLOPE = 0.2


def gnn_kernel(nc, x, src, dst, w_lin, b_lin, w_att, b_att, w_alpha, out):
    N, F = x.shape
    E = src.shape[0]
    NB = -(-N // P)
    TAIL = N - (NB - 1) * P
    T = -(-E // P)
    FULL = E // T
    REST = E - FULL * T
    WIDTH = 2048
    PIECE = WIDTH // 2
    LOCAL = WIDTH.bit_length() - 1
    PHASES = LOCAL + P.bit_length() - 1
    SROWS = E // WIDTH
    SREST = E - SROWS * WIDTH
    C = 4
    CHUNK = C * P
    PER = 2
    UNIT = CHUNK // PER
    UC = UNIT // P
    NUNITS = (E + NB * (UNIT - 1)) // UNIT
    NCH = -(-NUNITS // PER)
    SLOTS = 8
    AHEAD = 4
    U = 6
    W = (NCH + U + 2) * C
    R = 2 * F + 1
    GROUPS = NCH // U + 2
    PAD_ROW = NB * P
    PAD_PLACES = NB * (UNIT - 1)
    PROWS = -(-PAD_PLACES // WIDTH)
    PC = PROWS * WIDTH // P
    EDGE_ROWS = SROWS + 1
    SENDER_BITS = 13
    MARK = 1 << 30
    assert F == P and NCH == 427 and PROWS * WIDTH % P == 0
    assert (NCH + U + 2) * C <= WIDTH and (GROUPS + 1) * U * PER <= SLOTS * P and EDGE_ROWS + PROWS <= P
    assert PAD_ROW < 1 << SENDER_BITS and (NB + 1) * P <= 1 << 13

    RUNS = 2 * (PHASES - LOCAL) + 1
    def phase_of(run):
        return LOCAL + (run + 1) // 2
    starts_in, ends_in, now = [], [], 0
    for run in range(RUNS):
        starts_in.append(now)
        stages = LOCAL * (LOCAL + 1) // 2 if run == 0 else (run + 1) // 2 if run % 2 else LOCAL
        if run == RUNS - 1:
            stages -= UNIT.bit_length() - 1
        now = (now + stages) % 2
        ends_in.append(now)
        now = 1 - now
    PAD_AT = ends_in[0]
    assert starts_in[0] == PAD_AT == 0

    table = nc.dram_tensor("qv_table", [NB * P + 1, 2 * F], F32, kind="Internal").ap()
    pads_dram = nc.dram_tensor("pads", [P, PC], F32, kind="Internal").ap()
    blocks_dram = nc.dram_tensor("unit_blocks", [1, SLOTS * P], I32, kind="Internal").ap()

    with ExitStack() as ctx:
        def sb(name, shape, dt):
            return ctx.enter_context(nc.sbuf_tensor(name, shape, dt))

        def psum(name, shape, dt):
            return ctx.enter_context(nc.psum_tensor(name, shape, dt))

        def sem(name):
            return ctx.enter_context(nc.semaphore(name))

        identf = sb("identf", [P, P], F32)
        identb = sb("identb", [P, P], BF16)
        other = sb("other", [P, P], BF16)
        before = sb("before", [P, P], F32)
        onesf = sb("onesf", [P, P], F32)
        lane_i = sb("lane_i", [P, P], I32)
        lane = sb("lane", [P, P], BF16)
        part_i = sb("part_i", [P, 1], I32)
        bit_i = sb("bit_i", [P, LOCAL], I32)
        sign_of = sb("sign_of", [P, PHASES - LOCAL], F32)
        past_edges = sb("past_edges", [P, 1], F32)
        tail_sign = sb("tail_sign", [P, 1], F32)
        x_sb = sb("x_sb", [P, NB, F], F32)
        w3 = sb("w3", [P, 3 * F], F32)
        bias3 = sb("bias3", [1, 3 * F], F32)
        w_row = sb("w_row", [1, F], F32)
        w_col = sb("w_col", [P, 1], F32)
        w_cols = sb("w_cols", [P, P], F32)
        pad_row = sb("pad_row", [1, 2 * F], F32)
        x_turn = sb("x_turn", [P, 2, F], F32)
        xT = sb("xT", [P, 2, P], F32)
        qv_out = sb("qv_out", [P, 2, 2 * F], F32)
        parts_mem = sb("parts_mem", [P, NB * 3 * F], BF16)
        sums = sb("sums", [P, NB, F + 1], F32)
        low_peak = sb("low_peak", [P, NB], F32)
        keys_i = sb("keys_i", [P, 2, WIDTH], I32)
        keys = keys_i[:].bitcast(F32)
        recv = sb("recv", [P, T], I32)
        block_of = sb("block_of", [P, T], BF16)
        counting = sb("counting", [P, T], BF16)
        signs = sb("signs", [P, NB + 1], F32)
        thresholds = sb("thresholds", [P, NB + 1], F32)
        block_i = sb("block_i", [P, NB + 1], I32)
        sign_sums = sb("sign_sums", [P, NB + 1], F32)
        twice = sb("twice", [P, NB], F32)
        edges_of = sb("edges_of", [P, NB], F32)
        nb_f = sb("nb_f", [P, NB], F32)
        nb_i = sb("nb_i", [P, NB], I32)
        ends = sb("ends", [P, NB], F32)
        need = sb("need", [P, NB], F32)
        need_ends = sb("need_ends", [P, NB], F32)
        pad_i = sb("pad_i", [P, PC], I32)
        pad_work = sb("pad_work", [P, 2, PC], I32)
        pad_up = sb("pad_up", [P, PC], F32)
        pad_turn = sb("pad_turn", [P, PC], F32)
        pad_sign = sb("pad_sign", [P, PC], F32)
        pad_block = sb("pad_block", [P, 2, PC], F32)
        unit_i = sb("unit_i", [P, SLOTS], I32)
        unit_no = sb("unit_no", [P, SLOTS], F32)
        passed = sb("passed", [P, SLOTS, NB], F32)
        blk_f = sb("blk_f", [P, SLOTS], F32)
        blk_i = sb("blk_i", [P, SLOTS], I32)
        listed = sb("listed", [P, WIDTH], F32)
        senders = sb("senders", [P, WIDTH], I32)
        lane_bits = keys_i[:, 0, :]
        lanes = sb("lanes", [P, WIDTH], BF16)
        blocks = sb("blocks", [1, GROUPS, 2 * U * PER], I32)
        index = sb("index", [P, U, C], I32)
        rows = sb("rows", [P, U, C, R], F32)
        onehot = sb("onehot", [P, 2, C, P], BF16)
        onehotT = sb("onehotT", [P, 3, CHUNK], BF16)
        sloped = sb("sloped", [P, 2, CHUNK], F32)
        leaky = sb("leaky", [P, 2, CHUNK], F32)
        unit_low = sb("unit_low", [P, PER], F32)
        new_low = sb("new_low", [P, 2, PER], F32)
        growth = sb("growth", [P, 2, PER], F32)
        shrink = sb("shrink", [P, 2, PER], F32)
        weightsT = sb("weightsT", [P, 2, CHUNK], F32)
        weights = sb("weights", [P, 2, CHUNK], F32)
        recip = sb("recip", [P, NB], F32)
        spare = keys.rearrange("p a w -> p (a w)")
        stats = spare[:, 0:6 * NB].rearrange("p (b s) -> p b s", s=6)
        moments = spare[:, 6 * NB:8 * NB].rearrange("p (b s) -> p b s", s=2)

        turned_ps = psum("turned_ps", [P, WIDTH], F32)
        onehotT_ps = turned_ps[:, 0:2 * CHUNK].bitcast(BF16).rearrange("p (s c) -> p s c", s=2)
        weights_ps = turned_ps[:, 2 * CHUNK:3 * CHUNK]
        sums_ps = turned_ps[:, 3 * CHUNK:4 * CHUNK]
        hidden_ps = psum("hidden_ps", [P, 2, CHUNK], F32)
        masked_ps = psum("masked_ps", [P, 2, CHUNK], F32)
        unit_sums_ps = sums_ps.rearrange("p (i c) -> p i c", i=PER)[:, :, 0:F + 1]

        p_parts = parts_mem[:].rearrange("p (b s f) -> p b s f", s=3, f=F)
        elu_work = parts_mem[:].bitcast(F32)[:, 0:NB * F].rearrange("p (b f) -> p b f", f=F)
        p_f32 = sums[:, :, 0:F]

        filled = sem("filled")
        consts = sem("consts")
        consts_v = sem("consts_v")
        edges_in = sem("edges_in")
        x_in = sem("x_in")
        weights_in = sem("weights_in")
        prepared = sem("prepared")
        signed = sem("signed")
        totals_ps = sem("totals_ps")
        based = sem("based")
        pad_steps = sem("pad_steps")
        pads_ready = sem("pads_ready")
        pads_stored = sem("pads_stored")
        pads_in = sem("pads_in")
        compared = sem("compared")
        run_done = sem("run_done")
        turned = sem("turned")
        turn_out = sem("turn_out")
        cleared = sem("cleared")
        blk_ready = sem("blk_ready")
        blk_stored = sem("blk_stored")
        blk_loaded = sem("blk_loaded")
        x_staged = sem("x_staged")
        xT_ps = sem("xT_ps")
        xT_ready = sem("xT_ready")
        pqv_ps = sem("pqv_ps")
        p_ready = sem("p_ready")
        qv_ready = sem("qv_ready")
        qv_stored = [sem("qv_stored0"), sem("qv_stored1")]
        pad_row_ready = sem("pad_row_ready")
        pad_stored = sem("pad_stored")
        w_cols_ready = sem("w_cols_ready")
        unpacked = sem("unpacked")
        split = sem("split")
        indexed = sem("indexed")
        gathered = [sem(f"gathered{r}") for r in range(U)]
        onehot_ready = sem("onehot_ready")
        onehotT_done = sem("onehotT_done")
        onehotT_ready = sem("onehotT_ready")
        hidden_done = sem("hidden_done")
        sloped_ready = sem("sloped_ready")
        leaky_ready = sem("leaky_ready")
        masked_done = sem("masked_done")
        ones_ready = sem("ones_ready")
        unit_low_ready = sem("unit_low_ready")
        new_low_ready = sem("new_low_ready")
        growth_ready = sem("growth_ready")
        peak_ready = sem("peak_ready")
        weightsT_ready = sem("weightsT_ready")
        weights_done = sem("weights_done")
        weights_ready = sem("weights_ready")
        shrink_ready = sem("shrink_ready")
        chunk_sums_done = sem("chunk_sums_done")
        sums_ready = sem("sums_ready")
        finish = sem("finish")
        exp_done = sem("exp_done")
        sqrt_done = sem("sqrt_done")
        normed = sem("normed")
        stored = sem("stored")

        BODIES = NCH // U
        PAIRS_X = NB // 2
        assert NB % 2 == 1
        SLICES = PHASES - LOCAL
        BY = NB // SLICES
        LEAD = 3
        FILLS = 10
        assert SLICES * BY == NB

        def chunks(eng, step, of_body=None):
            def body(i, n):
                more = () if of_body is None else (of_body(i),)
                for j in range(n):
                    step(i, j, *more)

            body(0, U)
            with eng.Fori(1, BODIES) as i:
                body(i, U)
            body(BODIES, NCH - BODIES * U)

        def blocks_of(engine, i, first, n):
            at = blocks[:].rearrange("a g u -> a (g u)")[:, bass.ds(i * (2 * U * PER) + first * PER, n * PER)]
            return nc.values_load_multi_w_load_instructions(
                at, engines=(engine,), min_val=0, max_val=NB - 1,
                skip_runtime_bounds_check_because="they are counts of blocks, clamped to NB - 1")[1]

        def past(k, n):
            return not isinstance(k, int) or k >= n

        block = ctx.enter_context(nc.Block())

        @block.sync
        def _(sp):
            sp.wait_ge(filled, 2)
            sp.dma_start(recv[0:FULL, :], src[0:FULL * T].rearrange("(p c) -> p c", c=T)).then_inc(edges_in, 16)
            sp.dma_start(recv[FULL:FULL + 1, 0:REST],
                         src[FULL * T:E].rearrange("(p c) -> p c", p=1)).then_inc(edges_in, 16)
            for s, a in enumerate((src, dst)):
                sp.dma_start(keys_i[0:SROWS, s, :],
                             a[0:SROWS * WIDTH].rearrange("(p c) -> p c", c=WIDTH)).then_inc(edges_in, 16)
                sp.dma_start(keys_i[SROWS:SROWS + 1, s, 0:SREST],
                             a[SROWS * WIDTH:E].rearrange("(p c) -> p c", p=1)).then_inc(edges_in, 16)
            sp.wait_ge(filled, 4)
            sp.dma_start(w3[:, 0:F], w_att[0:F, :]).then_inc(weights_in, 16)
            sp.dma_start(w3[:, F:2 * F], w_att[F:2 * F, :]).then_inc(weights_in, 16)
            sp.dma_start(w3[:, 2 * F:3 * F], w_lin).then_inc(weights_in, 16)
            sp.dma_start(bias3[0:1, 0:F], b_att.rearrange("(a d) -> a d", a=1)).then_inc(weights_in, 16)
            sp.dma_start(bias3[0:1, 2 * F:3 * F], b_lin.rearrange("(a d) -> a d", a=1)).then_inc(weights_in, 16)
            sp.dma_start(w_row[:], w_alpha.rearrange("d a -> a d")).then_inc(weights_in, 16)
            sp.dma_start(w_col[:], w_alpha).then_inc(weights_in, 16)
            sp.dma_start(x_sb[:, 0:NB - 1, :],
                         x[0:(NB - 1) * P, :].rearrange("(b p) f -> p b f", p=P)).then_inc(x_in, 16)
            sp.dma_start(x_sb[0:TAIL, NB - 1, :], x[(NB - 1) * P:N, :]).then_inc(x_in, 16)
            def store_rows(b, j):
                sp.wait_ge(qv_ready, b + 1)
                sp.dma_start(table[bass.ds(b * P, P), :], qv_out[:, j, :]).then_inc(qv_stored[j], 16)

            with sp.Fori(0, PAIRS_X) as i:
                for j in (0, 1):
                    store_rows(i * 2 + j, j)
            store_rows(NB - 1, 0)
            sp.wait_ge(pad_row_ready, 3)
            sp.dma_start(table[PAD_ROW:PAD_ROW + 1, :], pad_row[:]).then_inc(pad_stored, 16)
            sp.wait_ge(blk_ready, 1)
            sp.dma_start(blocks_dram.rearrange("a (p g) -> (a p) g", g=SLOTS), blk_i[:]).then_inc(blk_stored, 16)
            sp.wait_ge(blk_stored, 16)
            for h in (0, 1):
                body = U * PER
                sp.dma_start(blocks[:, :, h * body:(h + 1) * body],
                             blocks_dram[:, h * body:(h + GROUPS) * body].rearrange("a (g u) -> a g u", u=body)).then_inc(blk_loaded, 16)
            sp.wait_ge(normed, NB)
            sp.dma_start(out[0:(NB - 1) * P, :].rearrange("(b p) f -> p b f", p=P),
                         x_sb[:, 0:NB - 1, :]).then_inc(stored, 16)
            sp.dma_start(out[(NB - 1) * P:N, :], x_sb[0:TAIL, NB - 1, :]).then_inc(stored, 16)
            sp.wait_ge(qv_stored[0], 16 * (PAIRS_X + 1))
            sp.wait_ge(qv_stored[1], 16 * PAIRS_X)
            sp.wait_ge(stored, 32)

        @block.gpsimd
        def _(pool):
            g = nc.gpsimd
            g.iota(lane_i[:], pattern=[[1, P]], base=0, channel_multiplier=0).then_inc(consts, 1)
            g.iota(block_i[:], pattern=[[1, NB + 1]], base=0, channel_multiplier=0).then_inc(consts, 1)
            g.iota(part_i[:], pattern=[[0, 1]], base=0, channel_multiplier=1).then_inc(consts, 1)
            g.iota(pad_i[:], pattern=[[1, PC]], base=0, channel_multiplier=PC).then_inc(consts, 1)
            g.iota(unit_i[:], pattern=[[1, SLOTS]], base=0, channel_multiplier=SLOTS).then_inc(consts, 1)
            pool.wait_ge(filled, 7)
            for t, one in ((identf, 1.0), (identb, 1.0), (other, 0.0)):
                g.affine_select(out=t[:], in_=t[:], compare_op=ALU.not_equal, fill=one, base=0,
                                pattern=[[-1, P]], channel_multiplier=1).then_inc(consts, 1)
            pool.wait_ge(pads_ready, 1)
            g.dma_start(pads_dram, pad_turn[:]).then_inc(pads_stored, 16)
            pool.wait_ge(pads_stored, 16)
            g.dma_start(keys[EDGE_ROWS:EDGE_ROWS + PROWS, PAD_AT, :],
                        pads_dram.rearrange("p c -> (p c)").rearrange("(q w) -> q w", w=WIDTH)).then_inc(pads_in, 16)
            pool.wait_ge(split, 5 * SLICES)
            g.memset(sums[:], 0.0).then_inc(cleared, 1)

            pool.wait_ge(qv_stored[0], 16 * (PAIRS_X + 1))
            pool.wait_ge(qv_stored[1], 16 * PAIRS_X)
            pool.wait_ge(pad_stored, 16)

            def gather(i, j):
                k = i * U + j
                pool.wait_ge(indexed, k + 1)
                if past(k, U):
                    pool.wait_ge(chunk_sums_done, k - U + 1)
                pool.nop(nofuse=True)
                for c in range(C):
                    g.indirect_dma_start(
                        out=rows[:, j, c, 0:2 * F], out_offset=None, in_=table,
                        in_offset=bass.IndirectOffsetOnAxis(ap=index[:, j, c:c + 1], axis=0),
                    ).then_inc(gathered[j], 16)

            chunks(pool, gather)
            for k in range(NCH, NCH + AHEAD):
                gather(k // U, k % U)

        @block.scalar
        def _(act):
            a = nc.scalar

            act.wait_ge(prepared, 2)
            act.wait_ge(consts_v, 3)
            with act.Fori(0, NB) as b:
                act.wait_ge(signed, b + 1)
                a.activation(counting[:], block_of[:], ACT.Sign, bias=thresholds[:, bass.ds(b + 1, 1)],
                             accum_out=signs[:, bass.ds(b + 1, 1)]).then_inc(signed, 1)

            act.wait_ge(x_in, 32)

            def stage_x(b, j):
                if past(b, 2):
                    act.wait_ge(xT_ps, b - 1)
                a.activation(x_turn[:, j, :], x_sb[:, bass.ds(b, 1), :].rearrange("p a f -> p (a f)"),
                             ACT.Copy).then_inc(x_staged, 1)

            def copy_xT(b, j):
                act.wait_ge(xT_ps, b + 1)
                a.activation(xT[:, j, :], masked_ps[:, j, 0:P], ACT.Copy).then_inc(xT_ready, 1)

            def copy_pqv(b, j, round):
                act.wait_ge(pqv_ps, b + 1)
                a.activation(p_f32[:, bass.ds(b, 1), :].rearrange("p a f -> p (a f)"),
                             hidden_ps[:, j, 0:F], ACT.Copy).then_inc(p_ready, 1)
                if past(b, 2):
                    act.wait_ge(qv_stored[j], round * 16)
                a.activation(qv_out[:, j, :], hidden_ps[:, j, F:3 * F], ACT.Copy).then_inc(qv_ready, 1)

            for b in range(4):
                stage_x(b, b % 2)
                if b >= 1:
                    copy_xT(b - 1, (b - 1) % 2)
                if b >= 2:
                    copy_pqv(b - 2, b % 2, 0)
            with act.Fori(1, PAIRS_X - 1) as i:
                for j in (0, 1):
                    stage_x(i * 2 + j + 2, j)
                    copy_xT(i * 2 + j + 1, 1 - j)
                    copy_pqv(i * 2 + j, j, i)
            for b in range(NB - 3, NB):
                if b + 2 < NB:
                    stage_x(b + 2, b % 2)
                if b + 1 < NB:
                    copy_xT(b + 1, (b + 1) % 2)
                copy_pqv(b, b % 2, b // 2)

            def piece_out(run, h):
                act.wait_ge(turned, 2 * run + h + 1)
                from_ps = turned_ps[:, h * PIECE:(h + 1) * PIECE]
                phase, to = phase_of(run), 1 - ends_in[run]
                if run == RUNS - 1:
                    a.activation(listed[:].rearrange("p (q c) -> p c q", q=P)[:, h * 8:(h + 1) * 8, :],
                                 from_ps.rearrange("p (c q) -> p c q", q=P), ACT.Copy).then_inc(turn_out, 1)
                elif run % 2:
                    scale = sign_of[:, phase - LOCAL:phase - LOCAL + 1] if phase < PHASES else 1.0
                    a.activation(keys[:, to, h * PIECE:(h + 1) * PIECE], from_ps,
                                 ACT.Identity, scale=scale).then_inc(turn_out, 1)
                else:
                    turn = dict(t=2, q=1 << (phase - LOCAL))
                    ins = from_ps.rearrange("p (g t q) -> p g t q", **turn)
                    outs = keys[:, to, h * PIECE:(h + 1) * PIECE].rearrange("p (g t q) -> p g t q", **turn)
                    a.activation(outs[:, :, 0, :], ins[:, :, 0, :], ACT.Identity)
                    a.activation(outs[:, :, 1, :], ins[:, :, 1, :], ACT.Identity, scale=-1.0).then_inc(turn_out, 1)

            for run in range(RUNS):
                for h in (0, 1):
                    piece_out(run, h)

            def stage_index(k, r, rounds):
                if past(k, U):
                    act.wait_ge(gathered[r], rounds * (16 * C))
                a.activation(index[:, r, :], senders[:, bass.ds(k * C, C)], ACT.Copy).then_inc(indexed, 1)

            def copy_onehotT(k, j):
                act.wait_ge(onehotT_done, k + 1)
                if past(k, 3):
                    act.wait_ge(masked_done, k - 2)
                a.activation(onehotT[:, j % 3, :], onehotT_ps[:, j % 2, 0:CHUNK], ACT.Copy).then_inc(onehotT_ready, 1)

            def slope(k, j):
                act.wait_ge(hidden_done, k + 1)
                if past(k, 2):
                    act.wait_ge(leaky_ready, k - 1)
                a.activation(sloped[:, j % 2, :], hidden_ps[:, j % 2, :], ACT.Copy, scale=SLOPE).then_inc(sloped_ready, 1)

            def weigh(k, j):
                if past(k, 2):
                    act.wait_ge(weights_done, k - 1)
                for i in range(PER):
                    unit = slice(i * UNIT, (i + 1) * UNIT)
                    act.wait_ge(new_low_ready, k * PER + i + 1)
                    last = a.activation(weightsT[:, j % 2, unit], masked_ps[:, j % 2, unit], ACT.Exp,
                                        bias=new_low[:, j % 2, i:i + 1])
                last.then_inc(weightsT_ready, 1)
                act.wait_ge(growth_ready, (k + 1) * PER)
                if past(k, 2):
                    act.wait_ge(sums_ready, (k - 1) * PER)
                a.activation(shrink[:, j % 2, :], growth[:, j % 2, :], ACT.Exp).then_inc(shrink_ready, 1)

            def copy_weights(k, j):
                act.wait_ge(weights_done, k + 1)
                if past(k, 2):
                    act.wait_ge(chunk_sums_done, k - 1)
                a.activation(weights[:, j % 2, :], weights_ps[:], ACT.Copy).then_inc(weights_ready, 1)

            act.wait_ge(unpacked, 1)
            for k in range(U):
                stage_index(k, k, 0)
            act.wait_ge(unpacked, 8)
            for k in range(4):
                copy_onehotT(k, k)
                if k >= 2:
                    weigh(k - 2, k - 2)
                if k <= 2:
                    slope(k, k)
            copy_weights(0, 0)
            stage_index(U, 0, 1)

            def step(i, j):
                k = i * U + j
                slope(k + 3, j + 3)
                copy_onehotT(k + 4, j + 4)
                copy_weights(k + 1, j + 1)
                weigh(k + 2, j + 2)
                stage_index(k + U + 1, (j + 1) % U, i + 1 + (j + 1) // U)

            chunks(act, step)

            act.wait_ge(finish, 4)
            a.activation(elu_work, elu_work, ACT.Exp).then_inc(exp_done, 1)
            act.wait_ge(finish, 9)
            a.activation(recip[:], recip[:], ACT.Sqrt).then_inc(sqrt_done, 1)

        @block.tensor
        def _(pe):
            t = nc.tensor
            pe.wait_ge(consts, 8)
            pe.wait_ge(filled, FILLS)
            pe.wait_ge(weights_in, 7 * 16)

            def turn_x(b, j):
                if past(b, 2):
                    pe.wait_ge(xT_ready, b - 1)
                pe.wait_ge(x_staged, b + 1)
                t.transpose(masked_ps[:, j, 0:P], x_turn[:, j, :], identf[:]).then_inc(xT_ps, 1)

            def project(b, j):
                pe.wait_ge(xT_ready, b + 1)
                if past(b, 2):
                    pe.wait_ge(qv_ready, b - 1)
                t.matmul(hidden_ps[:, j, 0:3 * F], xT[:, j, :], w3[:], start=True, stop=False)
                t.matmul(hidden_ps[:, j, 0:3 * F], onesf[0:1, :], bias3[:], start=False, stop=True).then_inc(pqv_ps, 1)

            pe.wait_ge(signed, NB + 1)
            t.matmul(sums_ps[:, 0:NB + 1], onesf[:], signs[:], start=True, stop=True).then_inc(totals_ps, 1)

            turn_x(0, 0)
            turn_x(1, 1)
            project(0, 0)

            def table_pairs(first, end):
                with pe.Fori(first, end) as i:
                    for j in (0, 1):
                        turn_x(i * 2 + j, j)
                        project(i * 2 + j - 1, 1 - j)

            table_pairs(1, PAIRS_X)
            turn_x(NB - 1, 0)
            project(NB - 2, 1)
            project(NB - 1, 0)

            pe.wait_ge(pads_in, 16)
            for run in range(RUNS):
                for h in (0, 1):
                    pe.wait_ge(run_done, 2 * run + h + 1)
                    if run:
                        pe.wait_ge(turn_out, 2 * run + h - 1)
                    for at in range(h * PIECE, (h + 1) * PIECE, P):
                        mm = t.transpose(turned_ps[:, at:at + P], keys[:, ends_in[run], at:at + P], identf[:])
                    mm.then_inc(turned, 1)

            def turn_onehot(k, j):
                pe.wait_ge(onehot_ready, k + 1)
                if past(k, 2):
                    pe.wait_ge(onehotT_ready, k - 1)
                for c in range(C):
                    mm = t.transpose(onehotT_ps[:, j % 2, c * P:(c + 1) * P], onehot[:, j % 2, c, :], identb[:])
                mm.then_inc(onehotT_done, 1)

            def hidden(k, j, rounds, of):
                pe.wait_ge(onehotT_ready, k + 1)
                if past(k, 2):
                    pe.wait_ge(leaky_ready, k - 1)
                whole = hidden_ps[:, j % 2, :]
                for i in range(PER):
                    unit = slice(i * UNIT, (i + 1) * UNIT)
                    for s in range(3):
                        t.matmul(whole[:, unit], p_parts[:, bass.ds(of[i], 1), s, :].rearrange("p a f -> p (a f)"),
                                 onehotT[:, j % 3, unit], start=(s == 0), stop=False, skip_group_check=True)
                    if i == 0:
                        pe.wait_ge(gathered[j % U], rounds * (16 * C))
                    for c in range(i * UC, (i + 1) * UC):
                        mm = t.matmul(whole[:, c * P:(c + 1) * P], rows[:, j % U, c, 0:F], identf[:],
                                      start=False, stop=(c == (i + 1) * UC - 1), skip_group_check=True)
                mm.then_inc(hidden_done, 1)

            def mask(k, j):
                pe.wait_ge(leaky_ready, k + 1)
                if past(k, 2):
                    pe.wait_ge(weightsT_ready, k - 1)
                whole = masked_ps[:, j % 2, :]
                t.matmul(whole, other[:], onehotT[:, j % 3, :], start=True, stop=False)
                t.matmul(whole, w_cols[:], leaky[:, j % 2, :], start=False, stop=True).then_inc(masked_done, 1)

            def turn_weights(k, j):
                pe.wait_ge(weightsT_ready, k + 1)
                if past(k, 1):
                    pe.wait_ge(weights_ready, k)
                for c in range(C):
                    mm = t.transpose(weights_ps[:, c * P:(c + 1) * P], weightsT[:, j % 2, c * P:(c + 1) * P], identf[:])
                mm.then_inc(weights_done, 1)

            def chunk_sums(k, j):
                pe.wait_ge(weights_ready, k + 1)
                pe.wait_ge(ones_ready, k + 1)
                if past(k, 1):
                    pe.wait_ge(sums_ready, k * PER)
                for c in range(C):
                    mm = t.matmul(unit_sums_ps[:, c // UC, :], weights[:, j % 2, c * P:(c + 1) * P],
                                  rows[:, j % U, c, F:R], start=(c % UC == 0), stop=(c % UC == UC - 1))
                mm.then_inc(chunk_sums_done, 1)

            pe.wait_ge(blk_loaded, 32)
            pe.wait_ge(split, 5 * SLICES)
            pe.wait_ge(w_cols_ready, 1)
            early = blocks_of(mybir.EngineType.PE, 0, 0, 4)
            for k in range(4):
                turn_onehot(k, k)
                hidden(k, k, 1, early[k * PER:(k + 1) * PER])
                if k >= 1:
                    mask(k - 1, k - 1)
            turn_weights(0, 0)

            def step(i, j, ahead):
                k = i * U + j
                turn_onehot(k + 4, j + 4)
                chunk_sums(k, j)
                turn_weights(k + 1, j + 1)
                hidden(k + 4, j + 4, i + 1 + (j + 4) // U, ahead[j * PER:(j + 1) * PER])
                mask(k + 3, j + 3)

            chunks(pe, step, lambda i: blocks_of(mybir.EngineType.PE, i, 4, U))

        @block.vector
        def _(dve):
            v = nc.vector
            v.memset(recv[:, REST:], NB * P).then_inc(filled, 1)
            v.memset(keys_i[:], PAD_ROW).then_inc(filled, 1)
            v.memset(x_sb[:, NB - 1, :], 0.0).then_inc(filled, 1)
            v.memset(bias3[:], 0.0).then_inc(filled, 1)
            v.memset(identf[:], 0.0).then_inc(filled, 1)
            v.memset(identb[:], 0.0).then_inc(filled, 1)
            v.memset(other[:], -BIG).then_inc(filled, 1)
            v.memset(onesf[:], 1.0).then_inc(filled, 1)
            v.memset(pad_row[:], 0.0).then_inc(filled, 1)
            v.memset(low_peak[:], 0.5 * BIG).then_inc(filled, 1)
            dve.wait_ge(consts, 5)
            v.tensor_copy(lane[:], lane_i[:]).then_inc(consts_v, 1)
            v.tensor_copy(unit_no[:], unit_i[:]).then_inc(consts_v, 1)
            v.tensor_scalar(thresholds[:], block_i[:], -1.0, 0.5, ALU.mult, ALU.add).then_inc(consts_v, 1)
            v.memset(signs[:, 0:1], float(T)).then_inc(signed, 1)
            for j in range(PHASES - LOCAL):
                v.tensor_scalar(bit_i[:, j:j + 1], part_i[:], j, 1, ALU.arith_shift_right,
                                ALU.bitwise_and).then_inc(consts_v, 1)
            v.tensor_scalar(past_edges[:], part_i[:], float(EDGE_ROWS), -2.0, ALU.is_ge, ALU.mult).then_inc(consts_v, 1)
            dve.wait_ge(consts_v, 4 + PHASES - LOCAL)
            v.tensor_scalar(sign_of[:], bit_i[:, 0:PHASES - LOCAL], -2.0, 1.0, ALU.mult, ALU.add).then_inc(consts_v, 1)
            v.tensor_tensor(tail_sign[:], past_edges[:], bit_i[:, 0:1], ALU.mult).then_inc(consts_v, 1)
            dve.wait_ge(consts_v, 6 + PHASES - LOCAL)
            v.tensor_scalar(tail_sign[:], tail_sign[:], 1.0, None, ALU.add).then_inc(consts_v, 1)

            dve.wait_ge(edges_in, 96)
            v.tensor_scalar(recv[:], recv[:], P.bit_length() - 1, None, ALU.arith_shift_right).then_inc(prepared, 1)
            dve.wait_ge(prepared, 1)
            v.tensor_copy(block_of[:], recv[:]).then_inc(prepared, 1)
            v.tensor_scalar(keys_i[:, 0, :], keys_i[:, 0, :], SENDER_BITS, MARK, ALU.logical_shift_left,
                            ALU.bitwise_or).then_inc(prepared, 1)
            dve.wait_ge(prepared, 3)
            v.tensor_tensor(keys_i[:, 0, :], keys_i[:, 0, :], keys_i[:, 1, :], ALU.bitwise_or).then_inc(prepared, 1)
            dve.wait_ge(prepared, 4)
            dve.wait_ge(consts_v, 7 + PHASES - LOCAL)
            v.tensor_scalar(keys[96:P, 0, :], keys[96:P, 0, :], tail_sign[96:P, :], None, ALU.mult).then_inc(prepared, 1)
            dve.wait_ge(prepared, 5)

            dve.wait_ge(weights_in, 7 * 16)
            dve.wait_ge(filled, FILLS)
            v.tensor_scalar(pad_row[:, 0:F], w_row[:], 0.0, -2.0 * LOW, ALU.is_gt, ALU.mult).then_inc(pad_row_ready, 1)
            dve.wait_ge(pad_row_ready, 1)
            v.tensor_scalar(pad_row[:, 0:F], pad_row[:, 0:F], LOW, None, ALU.add).then_inc(pad_row_ready, 2)
            v.tensor_scalar(w_cols[:], onesf[:], w_col[:], None, ALU.mult).then_inc(w_cols_ready, 1)

            def make_padding():
                dve.wait_ge(totals_ps, 1)
                v.tensor_copy(sign_sums[:], sums_ps[:, 0:NB + 1]).then_inc(based, 1)
                dve.wait_ge(based, 1)
                v.tensor_tensor(twice[:], sign_sums[:, 0:NB], sign_sums[:, 1:], ALU.subtract).then_inc(based, 1)
                dve.wait_ge(based, 2)
                v.tensor_scalar(edges_of[:], twice[:], 0.5, None, ALU.mult).then_inc(based, 1)
                v.tensor_scalar(nb_i[:], twice[:], 0.5, float(UNIT - 1), ALU.mult, ALU.add).then_inc(based, 1)
                dve.wait_ge(based, 4)
                v.tensor_scalar(nb_i[:], nb_i[:], UNIT.bit_length() - 1, None, ALU.arith_shift_right).then_inc(based, 1)
                dve.wait_ge(based, 5)
                v.tensor_copy(nb_f[:], nb_i[:]).then_inc(based, 1)
                dve.wait_ge(based, 6)
                v.tensor_tensor_scan(ends[:], nb_f[:], nb_f[:], 0.0, ALU.add, ALU.max).then_inc(based, 1)
                v.scalar_tensor_tensor(out=need[:], in0=nb_f[:], scalar=float(UNIT), in1=edges_of[:],
                                       op0=ALU.mult, op1=ALU.subtract).then_inc(based, 1)
                dve.wait_ge(based, 8)
                v.tensor_tensor_scan(need_ends[:], need[:], need[:], 0.0, ALU.add, ALU.max).then_inc(based, 1)
                v.tensor_tensor(passed[:], ends[:].unsqueeze(1).to_broadcast([P, SLOTS, NB]),
                                unit_no[:].unsqueeze(2).to_broadcast([P, SLOTS, NB]), ALU.is_le).then_inc(based, 1)
                dve.wait_ge(based, 10)
                v.tensor_reduce(blk_f[:], passed[:], AX_X, ALU.add).then_inc(based, 1)
                dve.wait_ge(based, 11)
                v.tensor_scalar(blk_i[:], blk_f[:], float(NB - 1), None, ALU.min).then_inc(blk_ready, 1)
                assert EDGE_ROWS % 2 == 1
                row_bit, col = pad_work[:, 0, :], pad_work[:, 1, :]
                v.tensor_scalar(row_bit, pad_i[:], LOCAL, 1, ALU.arith_shift_right, ALU.bitwise_and).then_inc(pad_steps, 1)
                v.tensor_scalar(col, pad_i[:], WIDTH - 1, None, ALU.bitwise_and).then_inc(pad_steps, 1)
                dve.wait_ge(pad_steps, 2)
                v.tensor_scalar(pad_up[:], col, -2.0, float(WIDTH - 1), ALU.mult, ALU.add).then_inc(pad_steps, 1)
                v.tensor_scalar(pad_turn[:], row_bit, -1.0, 1.0, ALU.mult, ALU.add).then_inc(pad_steps, 1)
                v.tensor_scalar(pad_sign[:], row_bit, 2.0, -1.0, ALU.mult, ALU.add).then_inc(pad_steps, 1)
                dve.wait_ge(pad_steps, 5)
                v.tensor_tensor(pad_up[:], pad_up[:], pad_turn[:], ALU.mult).then_inc(pad_steps, 1)
                dve.wait_ge(pad_steps, 6)
                v.tensor_tensor(pad_up[:], pad_up[:], pad_i[:], ALU.add).then_inc(pad_steps, 1)
                v.memset(pad_block[:], 0.0).then_inc(pad_steps, 1)
                dve.wait_ge(pad_steps, 8)
                def passes(b, i, wait):
                    if wait:
                        dve.wait_ge(pad_steps, b + 7)
                    v.scalar_tensor_tensor(out=pad_block[:, i, :], in0=pad_up[:], scalar=need_ends[:, bass.ds(b, 1)],
                                           in1=pad_block[:, i, :], op0=ALU.is_ge, op1=ALU.add).then_inc(pad_steps, 1)

                for i in (0, 1):
                    passes(i, i, False)
                with dve.Fori(1, NB // 2) as pair:
                    for i in (0, 1):
                        passes(pair * 2 + i, i, True)
                passes(NB - 1, 0, True)
                dve.wait_ge(pad_steps, NB + 8)
                v.tensor_tensor(row_bit, pad_block[:, 0, :], pad_block[:, 1, :], ALU.add).then_inc(pad_steps, 1)
                dve.wait_ge(pad_steps, NB + 9)
                v.tensor_scalar(col, row_bit, SENDER_BITS + P.bit_length() - 1, MARK | PAD_ROW,
                                ALU.logical_shift_left, ALU.bitwise_or).then_inc(pad_steps, 1)
                dve.wait_ge(pad_steps, NB + 10)
                v.tensor_tensor(pad_turn[:], col.bitcast(F32), pad_sign[:], ALU.mult).then_inc(pads_ready, 1)

            def split_p(s):
                if s == 0:
                    dve.wait_ge(p_ready, NB)
                at = slice(s * BY, (s + 1) * BY)
                for n in range(3):
                    v.tensor_copy(p_parts[:, at, n, :], p_f32[:, at, :]).then_inc(split, 1)
                    if n < 2:
                        dve.wait_ge(split, 5 * s + 2 * n + 1)
                        v.tensor_tensor(p_f32[:, at, :], p_f32[:, at, :], p_parts[:, at, n, :],
                                        ALU.subtract).then_inc(split, 1)
                        dve.wait_ge(split, 5 * s + 2 * n + 2)

            def compare(src, dst, dist):
                ins, outs = [x.rearrange("p (m t d) -> p m t d", t=2, d=dist) for x in (src, dst)]
                a, b = ins[:, :, 0, :], ins[:, :, 1, :]
                v.tensor_tensor(outs[:, :, 0, :], a, b, ALU.min)
                return v.tensor_tensor(outs[:, :, 1, :], a, b, ALU.max)

            def compare_groups(src, dst, dist, group, r):
                ins, outs = [x.rearrange("p (g r m t d) -> p g r m t d", r=2, m=group // (2 * dist), t=2, d=dist)
                             for x in (src, dst)]
                a, b = ins[:, :, r, :, 0, :], ins[:, :, r, :, 1, :]
                v.tensor_tensor(outs[:, :, r, :, r, :], a, b, ALU.min)
                return v.tensor_tensor(outs[:, :, r, :, 1 - r, :], a, b, ALU.max)

            done, now = 0, 0
            edge_rows = slice(0, EDGE_ROWS)
            for phase in range(1, LOCAL):
                if phase == LOCAL - 1:
                    make_padding()
                if done:
                    dve.wait_ge(compared, done)
                for stage in reversed(range(phase)):
                    for r in (0, 1):
                        if stage < phase - 1:
                            dve.wait_ge(compared, done - 1)
                        compare_groups(keys[edge_rows, now, :], keys[edge_rows, 1 - now, :], 1 << stage,
                                       1 << phase, r).then_inc(compared, 1)
                        done += 1
                    now = 1 - now
            dve.wait_ge(compared, done)
            half = keys[edge_rows, now, :]
            v.tensor_scalar(half, half, sign_of[edge_rows, 0:1], None, ALU.mult).then_inc(compared, 1)
            done += 1

            def within(rows, now, done, last=1):
                small = (PIECE // last).bit_length() - 1
                dve.wait_ge(compared, done)
                compare(keys[rows, now, :], keys[rows, 1 - now, :], PIECE).then_inc(compared, 1)
                now, done = 1 - now, done + 1
                left = [done, done]
                for n in range(small + LEAD):
                    for h, stage in ((0, n), (1, n - LEAD)):
                        if 0 <= stage < small:
                            at = slice(h * PIECE, (h + 1) * PIECE)
                            side = (now + stage) % 2
                            dve.wait_ge(compared, left[h])
                            end = stage == small - 1
                            compare(keys[rows, side, at], keys[rows, 1 - side, at], PIECE >> (stage + 1)).then_inc(
                                run_done if end else compared, 1)
                            if not end:
                                done += 1
                                left[h] = done
                return done

            done = within(edge_rows, now, done)
            for run in range(1, RUNS):
                phase, now = phase_of(run), starts_in[run]
                if run % 2:
                    stages = phase - LOCAL
                    groups = (0, 1) if phase < PHASES else (None,)
                    each = stages * len(groups) - 1
                    with dve.Fori(0, 2) as h:
                        side = [keys[:, n, bass.ds(h * PIECE, PIECE)] for n in (now, 1 - now)]
                        dve.wait_ge(turn_out, h + (2 * (run - 1) + 1))
                        for n in range(stages):
                            for i, r in enumerate(groups):
                                if n:
                                    dve.wait_ge(compared, h * each + (done + (n - 1) * len(groups) + i + 1))
                                args = side[n % 2], side[1 - n % 2], 1 << (stages - 1 - n)
                                last = compare(*args) if r is None else compare_groups(*args, 1 << stages, r)
                                last.then_inc(run_done if n == stages - 1 and r != 0 else compared, 1)
                    done += 2 * each
                else:
                    split_p(run // 2 - 1)
                    dve.wait_ge(turn_out, 2 * run)
                    done = within(slice(0, P), now, done, UNIT if phase == PHASES else 1)

            dve.wait_ge(turn_out, 2 * RUNS)
            bits = listed[:].bitcast(I32)
            FIRST = 16 * C
            for s, cols in enumerate((slice(0, FIRST), slice(FIRST, WIDTH))):
                v.tensor_scalar(senders[:, cols], bits[:, cols], (1 << SENDER_BITS) - 1, None,
                                ALU.bitwise_and).then_inc(unpacked, 1)
                v.tensor_scalar(lane_bits[:, cols], bits[:, cols], SENDER_BITS, P - 1, ALU.arith_shift_right,
                                ALU.bitwise_and).then_inc(unpacked, 1)
                dve.wait_ge(unpacked, 4 * s + 2)
                v.tensor_scalar(lanes[:, cols], senders[:, cols], float(PAD_ROW), float(P), ALU.is_ge,
                                ALU.mult).then_inc(unpacked, 1)
                dve.wait_ge(unpacked, 4 * s + 3)
                v.tensor_tensor(lanes[:, cols], lanes[:, cols], lane_bits[:, cols], ALU.add).then_inc(unpacked, 1)
            dve.wait_ge(unpacked, 8)
            dve.wait_ge(blk_loaded, 32)
            dve.wait_ge(cleared, 1)

            def make_onehot(k, j):
                if past(k, 2):
                    dve.wait_ge(onehotT_done, k - 1)
                v.tensor_tensor(onehot[:, j % 2], lane[:].unsqueeze(1).to_broadcast([P, C, P]),
                                lanes[:, bass.ds(k * C, C)].unsqueeze(2).to_broadcast([P, C, P]),
                                ALU.is_equal).then_inc(onehot_ready, 1)

            def leaky_relu(k, j):
                dve.wait_ge(sloped_ready, k + 1)
                if past(k, 2):
                    dve.wait_ge(masked_done, k - 1)
                v.tensor_tensor(leaky[:, j % 2, :], hidden_ps[:, j % 2, :], sloped[:, j % 2, :],
                                ALU.max).then_inc(leaky_ready, 1)

            def mark_ones(k, j):
                if past(k, U):
                    dve.wait_ge(chunk_sums_done, k - U + 1)
                v.tensor_scalar(rows[:, j % U, :, 2 * F], lanes[:, bass.ds(k * C, C)], float(P), None,
                                ALU.is_lt).then_inc(ones_ready, 1)

            def lowest(k, j):
                dve.wait_ge(masked_done, k + 1)
                if past(k, 1):
                    dve.wait_ge(new_low_ready, k * PER)
                v.tensor_reduce(unit_low[:], masked_ps[:, j % 2, :].rearrange("p (i e) -> p i e", i=PER), AX_X,
                                ALU.max, negate=True).then_inc(unit_low_ready, 1)

            def new_peak(k, j, i, of):
                dve.wait_ge(unit_low_ready, k + 1)
                if past(k, 2):
                    dve.wait_ge(weightsT_ready, k - 1)
                if past(k, 1) or i:
                    dve.wait_ge(peak_ready, k * PER + i)
                v.tensor_tensor(new_low[:, j % 2, i:i + 1], unit_low[:, i:i + 1], low_peak[:, bass.ds(of[i], 1)],
                                ALU.min).then_inc(new_low_ready, 1)

            def grow(k, j, i, of):
                dve.wait_ge(new_low_ready, k * PER + i + 1)
                if past(k, 2):
                    dve.wait_ge(shrink_ready, k - 1)
                v.tensor_tensor(growth[:, j % 2, i:i + 1], new_low[:, j % 2, i:i + 1], low_peak[:, bass.ds(of[i], 1)],
                                ALU.subtract).then_inc(growth_ready, 1)

            def set_peak(k, j, i, of):
                dve.wait_ge(growth_ready, k * PER + i + 1)
                new = new_low[:, j % 2, i:i + 1]
                v.tensor_tensor(low_peak[:, bass.ds(of[i], 1)], new, new, ALU.min).then_inc(peak_ready, 1)

            def add_sums(k, j, i, of):
                dve.wait_ge(chunk_sums_done, k + 1)
                dve.wait_ge(shrink_ready, k + 1)
                if past(k, 1) or i:
                    dve.wait_ge(sums_ready, k * PER + i)
                at = sums[:, bass.ds(of[i], 1), :].rearrange("p a f -> p (a f)")
                v.scalar_tensor_tensor(out=at, in0=at, scalar=shrink[:, j % 2, i:i + 1], in1=unit_sums_ps[:, i, :],
                                       op0=ALU.mult, op1=ALU.add).then_inc(sums_ready, 1)

            def raise_peak(k, of):
                lowest(k, k)
                for i in range(PER):
                    for part in (new_peak, grow, set_peak):
                        part(k, k, i, of)

            early = blocks_of(mybir.EngineType.DVE, 0, 0, 2)
            make_onehot(0, 0)
            make_onehot(1, 1)
            leaky_relu(0, 0)
            make_onehot(2, 2)
            leaky_relu(1, 1)
            for k in (0, 1):
                raise_peak(k, early[k * PER:(k + 1) * PER])
                mark_ones(k, k)
                make_onehot(k + 3, k + 3)
                if k == 0:
                    leaky_relu(2, 2)

            def step(i, j, of):
                k = i * U + j
                now, later = of[j * PER:(j + 1) * PER], of[(j + 2) * PER:(j + 3) * PER]
                lowest(k + 2, j + 2)
                make_onehot(k + 5, j + 5)
                new_peak(k + 2, j + 2, 0, later)
                mark_ones(k + 2, j + 2)
                grow(k + 2, j + 2, 0, later)
                leaky_relu(k + 3, j + 3)
                set_peak(k + 2, j + 2, 0, later)
                add_sums(k, j, 0, now)
                new_peak(k + 2, j + 2, 1, later)
                add_sums(k, j, 1, now)
                grow(k + 2, j + 2, 1, later)
                set_peak(k + 2, j + 2, 1, later)

            chunks(dve, step, lambda i: blocks_of(mybir.EngineType.DVE, i, 0, U + 2))

            dve.wait_ge(sums_ready, NCH * PER)
            v.tensor_scalar(recip[:], sums[:, :, F], 1e-12, None, ALU.max).then_inc(finish, 1)
            dve.wait_ge(finish, 1)
            v.reciprocal(recip[:], recip[:]).then_inc(finish, 1)
            dve.wait_ge(finish, 2)
            n = sums[:, :, 0:F]
            v.tensor_tensor(n, n, recip[:].unsqueeze(2).to_broadcast([P, NB, F]), ALU.mult).then_inc(finish, 1)
            dve.wait_ge(finish, 3)
            v.tensor_scalar(elu_work, n, 0.0, None, ALU.min).then_inc(finish, 1)
            v.scalar_tensor_tensor(out=x_sb[:], in0=n, scalar=0.0, in1=x_sb[:], op0=ALU.max, op1=ALU.add).then_inc(finish, 1)
            dve.wait_ge(finish, 5)
            dve.wait_ge(exp_done, 1)
            v.scalar_tensor_tensor(out=x_sb[:], in0=elu_work, scalar=-1.0, in1=x_sb[:], op0=ALU.add, op1=ALU.add).then_inc(finish, 1)
            dve.wait_ge(finish, 6)
            for b in range(NB):
                last = v.bn_stats(stats[:, b, :], x_sb[:, b, :])
            last.then_inc(finish, 1)
            dve.wait_ge(finish, 7)
            for b in range(NB):
                last = v.bn_aggr(moments[:, b, :], stats[:, b, :])
            last.then_inc(finish, 1)
            dve.wait_ge(finish, 8)
            v.tensor_scalar(recip[:], moments[:, :, 1], EPS, None, ALU.add).then_inc(finish, 1)
            dve.wait_ge(sqrt_done, 1)
            v.reciprocal(recip[:], recip[:]).then_inc(finish, 1)
            dve.wait_ge(finish, 10)
            for b in range(NB):
                v.tensor_scalar(x_sb[:, b, :], x_sb[:, b, :], moments[:, b, 0:1], recip[:, b:b + 1],
                                ALU.subtract, ALU.mult).then_inc(normed, 1)


_INS = ["x", "src", "dst", "L0_gnn_W_lin", "L0_gnn_b_lin", "L0_gnn_W_att", "L0_gnn_b_att", "L0_gnn_w_alpha"]


def kernel(**inputs):
    import numpy as _np
    import concourse.bacc as _bacc
    from concourse import mybir as _mybir
    from concourse.bass_utils import run_bass_kernel_spmd as _run

    nc = _bacc.Bacc("TRN2", target_bir_lowering=False, num_devices=1)
    arrays, args = {}, []
    for name in _INS:
        a = _np.ascontiguousarray(inputs[name])
        arrays[f"in_{name}"] = a
        args.append(nc.dram_tensor(f"in_{name}", a.shape, _mybir.dt.from_np(a.dtype), kind="ExternalInput").ap())
    shape = inputs["x"].shape
    args.append(nc.dram_tensor("out_0", shape, F32, kind="ExternalOutput").ap())
    gnn_kernel(nc, *args)
    r = _run(nc, [arrays], core_ids=[0])
    return r.results[0]["out_0"]
```

```python
from contextlib import ExitStack

import concourse.bass as bass
from concourse import mybir

F32 = mybir.dt.float32
BF16 = mybir.dt.bfloat16
I32 = mybir.dt.int32
U16 = mybir.dt.uint16
ALU = mybir.AluOpType
ACT = mybir.ActivationFunctionType
AX_X = mybir.AxisListType.X

P = 128
BIG = float(2.0 ** 100)
LOW = float(2.0 ** 90)
EPS = 1e-5
SLOPE = 0.2


def gnn_kernel(nc, x, src, dst, w_lin, b_lin, w_att, b_att, w_alpha, out):
    N, F = x.shape
    E = src.shape[0]
    NB = -(-N // P)
    TAIL = N - (NB - 1) * P
    T = -(-E // P)
    FULL = E // T
    REST = E - FULL * T
    WIDTH = 2048
    PIECE = WIDTH // 2
    LOCAL = WIDTH.bit_length() - 1
    PHASES = LOCAL + P.bit_length() - 1
    SROWS = E // WIDTH
    SREST = E - SROWS * WIDTH
    C = 4
    CHUNK = C * P
    PER = 2
    UNIT = CHUNK // PER
    UC = UNIT // P
    NUNITS = (E + NB * (UNIT - 1)) // UNIT
    NCH = -(-NUNITS // PER)
    SLOTS = 8
    AHEAD = 4
    U = 6
    R = 2 * F + 1
    GROUPS = NCH // U + 2
    PAD_ROW = NB * P
    PAD_PLACES = NB * (UNIT - 1)
    PROWS = -(-PAD_PLACES // WIDTH)
    PC = PROWS * WIDTH // P
    EDGE_ROWS = SROWS + 1
    SENDER_BITS = 13
    MARK = 1 << 30
    assert F == P and NCH == 427 and PROWS * WIDTH % P == 0
    assert (NCH + U + 2) * C <= WIDTH and (GROUPS + 1) * U * PER <= SLOTS * P and EDGE_ROWS + PROWS <= P
    assert PAD_ROW < 1 << SENDER_BITS and (NB + 1) * P <= 1 << 13

    RUNS = 2 * (PHASES - LOCAL)

    def phase_of(run):
        return LOCAL + (run + 1) // 2
    starts_in, ends_in, now = [], [], 0
    for run in range(RUNS):
        starts_in.append(now)
        stages = LOCAL * (LOCAL + 1) // 2 if run == 0 else (run + 1) // 2 if run % 2 else LOCAL
        if run == RUNS - 1:
            stages += LOCAL - (UNIT.bit_length() - 1)
        now = (now + stages) % 2
        ends_in.append(now)
        now = 1 - now
    PAD_AT = ends_in[0]
    assert starts_in[0] == PAD_AT == 0

    table = nc.dram_tensor("qv_table", [NB * P + 1, 2 * F], F32, kind="Internal").ap()
    pads_dram = nc.dram_tensor("pads", [P, PC], F32, kind="Internal").ap()
    blocks_dram = nc.dram_tensor("unit_blocks", [1, SLOTS * P], I32, kind="Internal").ap()

    with ExitStack() as ctx:
        def sb(name, shape, dt):
            return ctx.enter_context(nc.sbuf_tensor(name, shape, dt))

        def psum(name, shape, dt):
            return ctx.enter_context(nc.psum_tensor(name, shape, dt))

        def sem(name):
            return ctx.enter_context(nc.semaphore(name))

        identf = sb("identf", [P, P], F32)
        identb = sb("identb", [P, P], BF16)
        other = sb("other", [P, P], BF16)
        onesf = sb("onesf", [P, P], F32)
        lane_i = sb("lane_i", [P, P], I32)
        lane = sb("lane", [P, P], BF16)
        part_i = sb("part_i", [P, 1], I32)
        bit_i = sb("bit_i", [P, LOCAL], I32)
        sign_of = sb("sign_of", [P, PHASES - LOCAL], F32)
        past_edges = sb("past_edges", [P, 1], F32)
        tail_sign = sb("tail_sign", [P, 1], F32)
        x_sb = sb("x_sb", [P, NB, F], F32)
        w3 = sb("w3", [P, 3 * F], F32)
        bias3 = sb("bias3", [1, 3 * F], F32)
        w_row = sb("w_row", [1, F], F32)
        w_col = sb("w_col", [P, 1], F32)
        w_cols = sb("w_cols", [P, P], F32)
        pad_row = sb("pad_row", [1, 2 * F], F32)
        x_turn = sb("x_turn", [P, 2, F], F32)
        xT = sb("xT", [P, 2, P], F32)
        qv_out = sb("qv_out", [P, 2, 2 * F], F32)
        parts_mem = sb("parts_mem", [P, NB * 3 * F], BF16)
        sums = sb("sums", [P, NB, F + 1], F32)
        low_peak = sb("low_peak", [P, NB], F32)
        keys_i = sb("keys_i", [P, 2, WIDTH], I32)
        keys = keys_i[:].bitcast(F32)
        recv = sb("recv", [P, T], I32)
        block_of = sb("block_of", [P, T], BF16)
        counting = sb("counting", [P, T], BF16)
        signs = sb("signs", [P, NB + 1], F32)
        thresholds = sb("thresholds", [P, NB + 1], F32)
        block_i = sb("block_i", [P, NB + 1], I32)
        sign_sums = sb("sign_sums", [P, NB + 1], F32)
        twice = sb("twice", [P, NB], F32)
        edges_of = sb("edges_of", [P, NB], F32)
        nb_f = sb("nb_f", [P, NB], F32)
        nb_i = sb("nb_i", [P, NB], I32)
        ends = sb("ends", [P, NB], F32)
        need = sb("need", [P, NB], F32)
        need_ends = sb("need_ends", [P, NB], F32)
        pad_i = sb("pad_i", [P, PC], I32)
        pad_work = sb("pad_work", [P, 2, PC], I32)
        pad_up = sb("pad_up", [P, PC], F32)
        pad_turn = sb("pad_turn", [P, PC], F32)
        pad_sign = sb("pad_sign", [P, PC], F32)
        pad_block = sb("pad_block", [P, 2, PC], F32)
        unit_i = sb("unit_i", [P, SLOTS], I32)
        unit_no = sb("unit_no", [P, SLOTS], F32)
        passed = sb("passed", [P, SLOTS, NB], F32)
        blk_f = sb("blk_f", [P, SLOTS], F32)
        blk_i = sb("blk_i", [P, SLOTS], I32)
        senders = sb("senders", [P, WIDTH], I32)
        lane_bits = keys_i[:, 1 - ends_in[-1], :]
        lanes = sb("lanes", [P, WIDTH], BF16)
        blocks = sb("blocks", [1, GROUPS, 2 * U * PER], I32)
        index = sb("index", [P, U, C], I32)
        rows = sb("rows", [P, U, C, R], F32)
        onehot = sb("onehot", [P, 2, C, P], BF16)
        onehotT = sb("onehotT", [P, 3, CHUNK], BF16)
        sloped = sb("sloped", [P, 2, CHUNK], F32)
        leaky = sb("leaky", [P, 2, CHUNK], F32)
        unit_low = sb("unit_low", [P, PER], F32)
        new_low = sb("new_low", [P, 2, PER], F32)
        growth = sb("growth", [P, 2, PER], F32)
        shrink = sb("shrink", [P, 2, PER], F32)
        weightsT = sb("weightsT", [P, 2, CHUNK], F32)
        weights = sb("weights", [P, 2, CHUNK], F32)
        recip = sb("recip", [P, NB], F32)
        offset = sb("offset", [P, NB], F32)
        spare = keys.rearrange("p a w -> p (a w)")
        stats = spare[:, 0:6 * NB].rearrange("p (b s) -> p b s", s=6)
        moments = spare[:, 6 * NB:8 * NB].rearrange("p (b s) -> p b s", s=2)

        turned_ps = psum("turned_ps", [P, WIDTH], F32)
        onehotT_ps = turned_ps[:, 0:2 * CHUNK].bitcast(BF16).rearrange("p (s c) -> p s c", s=2)
        weights_ps = turned_ps[:, 2 * CHUNK:3 * CHUNK]
        sums_ps = turned_ps[:, 3 * CHUNK:4 * CHUNK]
        hidden_ps = psum("hidden_ps", [P, 2, CHUNK], F32)
        masked_ps = psum("masked_ps", [P, 2, CHUNK], F32)
        unit_sums_ps = sums_ps.rearrange("p (i c) -> p i c", i=PER)[:, :, 0:F + 1]

        p_parts = parts_mem[:].rearrange("p (b s f) -> p b s f", s=3, f=F)
        elu_work = parts_mem[:].bitcast(F32)[:, 0:NB * F].rearrange("p (b f) -> p b f", f=F)
        p_f32 = sums[:, :, 0:F]

        filled = sem("filled")
        consts = sem("consts")
        consts_v = sem("consts_v")
        edges_in = sem("edges_in")
        x_in = sem("x_in")
        weights_in = sem("weights_in")
        prepared = sem("prepared")
        signed = sem("signed")
        totals_ps = sem("totals_ps")
        based = sem("based")
        pad_steps = sem("pad_steps")
        pads_ready = sem("pads_ready")
        pads_stored = sem("pads_stored")
        pads_in = sem("pads_in")
        compared = sem("compared")
        run_done = sem("run_done")
        turned = sem("turned")
        turn_out = sem("turn_out")
        cleared = sem("cleared")
        blk_ready = sem("blk_ready")
        blk_stored = sem("blk_stored")
        blk_loaded = sem("blk_loaded")
        x_staged = sem("x_staged")
        xT_ps = sem("xT_ps")
        xT_ready = sem("xT_ready")
        pqv_ps = sem("pqv_ps")
        p_ready = sem("p_ready")
        qv_ready = sem("qv_ready")
        qv_stored = [sem("qv_stored0"), sem("qv_stored1")]
        pad_row_ready = sem("pad_row_ready")
        pad_stored = sem("pad_stored")
        w_cols_ready = sem("w_cols_ready")
        unpacked = sem("unpacked")
        lessened = sem("lessened")
        split = sem("split")
        indexed = sem("indexed")
        gathered = [sem(f"gathered{r}") for r in range(U)]
        onehot_ready = sem("onehot_ready")
        onehotT_done = sem("onehotT_done")
        onehotT_ready = sem("onehotT_ready")
        hidden_done = sem("hidden_done")
        sloped_ready = sem("sloped_ready")
        leaky_ready = sem("leaky_ready")
        masked_done = sem("masked_done")
        ones_ready = sem("ones_ready")
        unit_low_ready = sem("unit_low_ready")
        new_low_ready = sem("new_low_ready")
        growth_ready = sem("growth_ready")
        peak_ready = sem("peak_ready")
        weightsT_ready = sem("weightsT_ready")
        weights_done = sem("weights_done")
        weights_ready = sem("weights_ready")
        shrink_ready = sem("shrink_ready")
        chunk_sums_done = sem("chunk_sums_done")
        sums_ready = sem("sums_ready")
        x_less = sem("x_less")
        finish = sem("finish")
        divided = sem("divided")
        exp_done = sem("exp_done")
        mixed = sem("mixed")
        measured = sem("measured")
        spread = sem("spread")
        sqrt_done = sem("sqrt_done")
        normed_a = sem("normed_a")
        normed_v = sem("normed_v")
        stored = sem("stored")

        BODIES = NCH // U
        PAIRS_X = NB // 2
        assert NB % 2 == 1
        SLICES = PHASES - LOCAL
        BY = NB // SLICES
        LEAD = 2
        FILLS = 10
        assert SLICES * BY == NB
        SPLITS = [[(0, 0), (1, 0)], [(2, 0), (0, 1)], [(3, 0), (1, 1)], [(4, 0), (5, 0), (2, 1)],
                  [(6, 0), (3, 1), (4, 1)], [(5, 1), (6, 1)]]
        ALL_SPLITS = sum(len(step) for step in SPLITS)
        assert len(SPLITS) == PHASES - LOCAL - 1 and ALL_SPLITS == 2 * SLICES
        BATCHES = [(0, 3), (3, 6), (6, 7)]
        LAST_V = 3
        assert BATCHES[-1][1] * BY == NB

        def chunks(eng, step, of_body=None):
            def body(i, n):
                more = () if of_body is None else (of_body(i),)
                for j in range(n):
                    step(i, j, *more)

            body(0, U)
            with eng.Fori(1, BODIES) as i:
                body(i, U)
            body(BODIES, NCH - BODIES * U)

        def blocks_of(engine, i, first, n):
            at = blocks[:].rearrange("a g u -> a (g u)")[:, bass.ds(i * (2 * U * PER) + first * PER, n * PER)]
            return nc.values_load_multi_w_load_instructions(
                at, engines=(engine,), min_val=0, max_val=NB - 1,
                skip_runtime_bounds_check_because="they are counts of blocks, clamped to NB - 1")[1]

        def past(k, n):
            return not isinstance(k, int) or k >= n

        block = ctx.enter_context(nc.Block())

        @block.sync
        def _(sp):
            LAST = 96
            sp.dma_start(recv[0:LAST, :], src[0:LAST * T].rearrange("(p c) -> p c", c=T)).then_inc(edges_in, 16)
            for s, a in enumerate((src, dst)):
                sp.dma_start(keys_i[0:LAST, s, :],
                             a[0:LAST * WIDTH].rearrange("(p c) -> p c", c=WIDTH)).then_inc(edges_in, 16)
            sp.wait_ge(filled, 2)
            sp.dma_start(recv[LAST:FULL, :], src[LAST * T:FULL * T].rearrange("(p c) -> p c", c=T)).then_inc(edges_in, 16)
            sp.dma_start(recv[FULL:FULL + 1, 0:REST],
                         src[FULL * T:E].rearrange("(p c) -> p c", p=1)).then_inc(edges_in, 16)
            for s, a in enumerate((src, dst)):
                sp.dma_start(keys_i[LAST:SROWS, s, :],
                             a[LAST * WIDTH:SROWS * WIDTH].rearrange("(p c) -> p c", c=WIDTH)).then_inc(edges_in, 16)
                sp.dma_start(keys_i[SROWS:SROWS + 1, s, 0:SREST],
                             a[SROWS * WIDTH:E].rearrange("(p c) -> p c", p=1)).then_inc(edges_in, 16)
            sp.wait_ge(filled, 4)
            sp.dma_start(w3[:, 0:F], w_att[0:F, :]).then_inc(weights_in, 16)
            sp.dma_start(w3[:, F:2 * F], w_att[F:2 * F, :]).then_inc(weights_in, 16)
            sp.dma_start(w3[:, 2 * F:3 * F], w_lin).then_inc(weights_in, 16)
            sp.dma_start(bias3[0:1, 0:F], b_att.rearrange("(a d) -> a d", a=1)).then_inc(weights_in, 16)
            sp.dma_start(bias3[0:1, 2 * F:3 * F], b_lin.rearrange("(a d) -> a d", a=1)).then_inc(weights_in, 16)
            sp.dma_start(w_row[:], w_alpha.rearrange("d a -> a d")).then_inc(weights_in, 16)
            sp.dma_start(w_col[:], w_alpha).then_inc(weights_in, 16)
            sp.dma_start(x_sb[:, 0:NB - 1, :],
                         x[0:(NB - 1) * P, :].rearrange("(b p) f -> p b f", p=P)).then_inc(x_in, 16)
            sp.dma_start(x_sb[0:TAIL, NB - 1, :], x[(NB - 1) * P:N, :]).then_inc(x_in, 16)
            def store_rows(b, j):
                sp.wait_ge(qv_ready, b + 1)
                sp.dma_start(table[bass.ds(b * P, P), :], qv_out[:, j, :]).then_inc(qv_stored[j], 16)

            with sp.Fori(0, PAIRS_X) as i:
                for j in (0, 1):
                    store_rows(i * 2 + j, j)
            store_rows(NB - 1, 0)
            sp.wait_ge(pad_row_ready, 3)
            sp.dma_start(table[PAD_ROW:PAD_ROW + 1, :], pad_row[:]).then_inc(pad_stored, 16)
            sp.wait_ge(blk_ready, 1)
            sp.dma_start(blocks_dram.rearrange("a (p g) -> (a p) g", g=SLOTS), blk_i[:]).then_inc(blk_stored, 16)
            sp.wait_ge(blk_stored, 16)
            for h in (0, 1):
                body = U * PER
                sp.dma_start(blocks[:, :, h * body:(h + 1) * body],
                             blocks_dram[:, h * body:(h + GROUPS) * body].rearrange("a (g u) -> a g u", u=body)).then_inc(blk_loaded, 16)
            for first, end in BATCHES:
                last = min(end * BY, NB - LAST_V)
                sp.wait_ge(normed_a, last)
                sp.dma_start(out[first * BY * P:last * P, :].rearrange("(b p) f -> p b f", p=P),
                             x_sb[:, first * BY:last, :]).then_inc(stored, 16)
            sp.wait_ge(normed_v, LAST_V)
            sp.dma_start(out[(NB - LAST_V) * P:(NB - 1) * P, :].rearrange("(b p) f -> p b f", p=P),
                         x_sb[:, NB - LAST_V:NB - 1, :]).then_inc(stored, 16)
            sp.dma_start(out[(NB - 1) * P:N, :], x_sb[0:TAIL, NB - 1, :]).then_inc(stored, 16)
            sp.wait_ge(qv_stored[0], 16 * (PAIRS_X + 1))
            sp.wait_ge(qv_stored[1], 16 * PAIRS_X)
            sp.wait_ge(stored, 16 * (len(BATCHES) + 2))

        @block.gpsimd
        def _(pool):
            g = nc.gpsimd
            g.iota(lane_i[:], pattern=[[1, P]], base=0, channel_multiplier=0).then_inc(consts, 1)
            g.iota(block_i[:], pattern=[[1, NB + 1]], base=0, channel_multiplier=0).then_inc(consts, 1)
            g.iota(part_i[:], pattern=[[0, 1]], base=0, channel_multiplier=1).then_inc(consts, 1)
            g.iota(pad_i[:], pattern=[[1, PC]], base=0, channel_multiplier=PC).then_inc(consts, 1)
            g.iota(unit_i[:], pattern=[[1, SLOTS]], base=0, channel_multiplier=SLOTS).then_inc(consts, 1)
            pool.wait_ge(filled, 7)
            for t, one in ((identf, 1.0), (identb, 1.0), (other, 0.0)):
                g.affine_select(out=t[:], in_=t[:], compare_op=ALU.not_equal, fill=one, base=0,
                                pattern=[[-1, P]], channel_multiplier=1).then_inc(consts, 1)
            pool.wait_ge(pads_ready, 1)
            g.dma_start(pads_dram, pad_turn[:]).then_inc(pads_stored, 16)
            pool.wait_ge(pads_stored, 16)
            g.dma_start(keys[EDGE_ROWS:EDGE_ROWS + PROWS, PAD_AT, :],
                        pads_dram.rearrange("p c -> (p c)").rearrange("(q w) -> q w", w=WIDTH)).then_inc(pads_in, 16)
            pool.wait_ge(split, 1 + ALL_SPLITS)
            g.memset(sums[:], 0.0).then_inc(cleared, 1)

            pool.wait_ge(qv_stored[0], 16 * (PAIRS_X + 1))
            pool.wait_ge(qv_stored[1], 16 * PAIRS_X)
            pool.wait_ge(pad_stored, 16)

            def gather(i, j):
                k = i * U + j
                pool.wait_ge(indexed, k + 1)
                if past(k, U):
                    pool.wait_ge(chunk_sums_done, k - U + 1)
                pool.nop(nofuse=True)
                for c in range(C):
                    g.indirect_dma_start(
                        out=rows[:, j, c, 0:2 * F], out_offset=None, in_=table,
                        in_offset=bass.IndirectOffsetOnAxis(ap=index[:, j, c:c + 1], axis=0),
                    ).then_inc(gathered[j], 16)

            chunks(pool, gather)
            for k in range(NCH, NCH + AHEAD):
                gather(k // U, k % U)

        @block.scalar
        def _(act):
            a = nc.scalar

            act.wait_ge(prepared, 2)
            act.wait_ge(consts_v, 3)

            def count_pass(b):
                act.wait_ge(signed, b + 1)
                at = bass.ds(b + 1, 1)
                a.activation(counting[:], block_of[:], ACT.Sign, bias=thresholds[:, at],
                             accum_out=signs[:, at]).then_inc(signed, 1)

            act.wait_ge(x_in, 32)

            def stage_x(b, j):
                if past(b, 2):
                    act.wait_ge(xT_ps, b - 1)
                a.activation(x_turn[:, j, :], x_sb[:, bass.ds(b, 1), :].rearrange("p a f -> p (a f)"),
                             ACT.Copy).then_inc(x_staged, 1)

            def copy_xT(b, j):
                act.wait_ge(xT_ps, b + 1)
                a.activation(xT[:, j, :], masked_ps[:, j, 0:P], ACT.Copy).then_inc(xT_ready, 1)

            def copy_pqv(b, j, round):
                act.wait_ge(pqv_ps, b + 1)
                a.activation(p_f32[:, bass.ds(b, 1), :].rearrange("p a f -> p (a f)"),
                             hidden_ps[:, j, 0:F], ACT.Copy).then_inc(p_ready, 1)
                if past(b, 2):
                    act.wait_ge(qv_stored[j], round * 16)
                a.activation(qv_out[:, j, :], hidden_ps[:, j, F:3 * F], ACT.Copy).then_inc(qv_ready, 1)

            for b in range(4):
                stage_x(b, b % 2)
                if b >= 1:
                    copy_xT(b - 1, (b - 1) % 2)
                if b >= 2:
                    copy_pqv(b - 2, b % 2, 0)
                    count_pass(b - 2)
            with act.Fori(1, PAIRS_X - 1) as i:
                for j in (0, 1):
                    stage_x(i * 2 + j + 2, j)
                    copy_xT(i * 2 + j + 1, 1 - j)
                    copy_pqv(i * 2 + j, j, i)
                    count_pass(i * 2 + j)
            for b in range(NB - 3, NB):
                if b + 2 < NB:
                    stage_x(b + 2, b % 2)
                if b + 1 < NB:
                    copy_xT(b + 1, (b + 1) % 2)
                copy_pqv(b, b % 2, b // 2)
                count_pass(b)

            act.wait_ge(x_staged, NB)
            act.wait_ge(xT_ps, NB)
            a.activation(x_sb[:], x_sb[:], ACT.Copy, bias=-1.0).then_inc(x_less, 1)

            def piece_out(run, h):
                act.wait_ge(turned, 2 * run + h + 1)
                from_ps = turned_ps[:, h * PIECE:(h + 1) * PIECE]
                phase, to = phase_of(run), 1 - ends_in[run]
                if run % 2:
                    a.activation(keys[:, to, h * PIECE:(h + 1) * PIECE], from_ps, ACT.Identity,
                                 scale=sign_of[:, phase - LOCAL:phase - LOCAL + 1]).then_inc(turn_out, 1)
                else:
                    turn = dict(t=2, q=1 << (phase - LOCAL))
                    ins = from_ps.rearrange("p (g t q) -> p g t q", **turn)
                    outs = keys[:, to, h * PIECE:(h + 1) * PIECE].rearrange("p (g t q) -> p g t q", **turn)
                    a.activation(outs[:, :, 0, :], ins[:, :, 0, :], ACT.Identity)
                    a.activation(outs[:, :, 1, :], ins[:, :, 1, :], ACT.Identity, scale=-1.0).then_inc(turn_out, 1)

            act.wait_ge(p_ready, NB)
            a.activation(p_parts[:, :, 0, :], p_f32, ACT.Copy).then_inc(split, 1)
            lessenings = 0
            for run in range(RUNS - 1):
                for h in (0, 1):
                    piece_out(run, h)
                if run % 2:
                    for s, part in SPLITS[run // 2]:
                        lessenings += 1
                        act.wait_ge(lessened, lessenings)
                        at = slice(s * BY, (s + 1) * BY)
                        a.activation(p_parts[:, at, part + 1, :], p_f32[:, at, :], ACT.Copy).then_inc(split, 1)

            def stage_index(k, r, rounds):
                if past(k, U):
                    act.wait_ge(gathered[r], rounds * (16 * C))
                a.activation(index[:, r, :], senders[:, bass.ds(k * C, C)], ACT.Copy).then_inc(indexed, 1)

            def copy_onehotT(k, j):
                act.wait_ge(onehotT_done, k + 1)
                if past(k, 3):
                    act.wait_ge(masked_done, k - 2)
                a.activation(onehotT[:, j % 3, :], onehotT_ps[:, j % 2, 0:CHUNK], ACT.Copy).then_inc(onehotT_ready, 1)

            def slope(k, j):
                act.wait_ge(hidden_done, k + 1)
                if past(k, 2):
                    act.wait_ge(leaky_ready, k - 1)
                a.activation(sloped[:, j % 2, :], hidden_ps[:, j % 2, :], ACT.Copy, scale=SLOPE).then_inc(sloped_ready, 1)

            def weigh(k, j):
                if past(k, 2):
                    act.wait_ge(weights_done, k - 1)
                for i in range(PER):
                    unit = slice(i * UNIT, (i + 1) * UNIT)
                    act.wait_ge(new_low_ready, k * PER + i + 1)
                    last = a.activation(weightsT[:, j % 2, unit], masked_ps[:, j % 2, unit], ACT.Exp,
                                        bias=new_low[:, j % 2, i:i + 1])
                last.then_inc(weightsT_ready, 1)
                act.wait_ge(growth_ready, (k + 1) * PER)
                if past(k, 2):
                    act.wait_ge(sums_ready, (k - 1) * PER)
                a.activation(shrink[:, j % 2, :], growth[:, j % 2, :], ACT.Exp).then_inc(shrink_ready, 1)

            def copy_weights(k, j):
                act.wait_ge(weights_done, k + 1)
                if past(k, 2):
                    act.wait_ge(chunk_sums_done, k - 1)
                a.activation(weights[:, j % 2, :], weights_ps[:], ACT.Copy).then_inc(weights_ready, 1)

            act.wait_ge(unpacked, 1)
            for k in range(U):
                stage_index(k, k, 0)
            act.wait_ge(unpacked, 8)
            for k in range(4):
                copy_onehotT(k, k)
                if k >= 2:
                    weigh(k - 2, k - 2)
                if k <= 2:
                    slope(k, k)
            copy_weights(0, 0)
            stage_index(U, 0, 1)

            def step(i, j):
                k = i * U + j
                slope(k + 3, j + 3)
                copy_onehotT(k + 4, j + 4)
                copy_weights(k + 1, j + 1)
                weigh(k + 2, j + 2)
                stage_index(k + U + 1, (j + 1) % U, i + 1 + (j + 1) // U)

            chunks(act, step)

            act.wait_ge(hidden_done, NCH + AHEAD)
            for g in range(SLICES):
                at = slice(g * BY, (g + 1) * BY)
                act.wait_ge(divided, g + 1)
                a.activation(elu_work[:, at, :], sums[:, at, 0:F], ACT.Exp).then_inc(exp_done, 1)
            for n, (first, end) in enumerate(BATCHES):
                at = slice(first * BY, end * BY)
                act.wait_ge(spread, 3 * n + 1)
                a.activation(recip[:, at], recip[:, at], ACT.Sqrt).then_inc(sqrt_done, 1)
                act.wait_ge(spread, 3 * n + 3)
                for b in range(first * BY, min(end * BY, NB - LAST_V)):
                    a.activation(x_sb[:, b, :], x_sb[:, b, :], ACT.Identity, scale=recip[:, b:b + 1],
                                 bias=offset[:, b:b + 1]).then_inc(normed_a, 1)

        @block.tensor
        def _(pe):
            t = nc.tensor
            pe.wait_ge(consts, 8)
            pe.wait_ge(filled, FILLS)
            pe.wait_ge(weights_in, 7 * 16)

            def turn_x(b, j):
                if past(b, 2):
                    pe.wait_ge(xT_ready, b - 1)
                pe.wait_ge(x_staged, b + 1)
                t.transpose(masked_ps[:, j, 0:P], x_turn[:, j, :], identf[:]).then_inc(xT_ps, 1)

            def project(b, j):
                pe.wait_ge(xT_ready, b + 1)
                if past(b, 2):
                    pe.wait_ge(qv_ready, b - 1)
                t.matmul(hidden_ps[:, j, 0:3 * F], xT[:, j, :], w3[:], start=True, stop=False)
                t.matmul(hidden_ps[:, j, 0:3 * F], onesf[0:1, :], bias3[:], start=False, stop=True).then_inc(pqv_ps, 1)

            turn_x(0, 0)
            turn_x(1, 1)
            project(0, 0)

            def table_pairs(first, end):
                with pe.Fori(first, end) as i:
                    for j in (0, 1):
                        turn_x(i * 2 + j, j)
                        project(i * 2 + j - 1, 1 - j)

            table_pairs(1, PAIRS_X)
            turn_x(NB - 1, 0)
            project(NB - 2, 1)
            project(NB - 1, 0)

            pe.wait_ge(signed, NB + 1)
            t.matmul(sums_ps[:, 0:NB + 1], onesf[:], signs[:], start=True, stop=True).then_inc(totals_ps, 1)

            pe.wait_ge(pads_in, 16)
            for run in range(RUNS - 1):
                for h in (0, 1):
                    pe.wait_ge(run_done, 2 * run + h + 1)
                    if run:
                        pe.wait_ge(turn_out, 2 * run + h - 1)
                    for at in range(h * PIECE, (h + 1) * PIECE, P):
                        mm = t.transpose(turned_ps[:, at:at + P], keys[:, ends_in[run], at:at + P], identf[:])
                    mm.then_inc(turned, 1)

            def turn_onehot(k, j):
                pe.wait_ge(onehot_ready, k + 1)
                if past(k, 2):
                    pe.wait_ge(onehotT_ready, k - 1)
                for c in range(C):
                    mm = t.transpose(onehotT_ps[:, j % 2, c * P:(c + 1) * P], onehot[:, j % 2, c, :], identb[:])
                mm.then_inc(onehotT_done, 1)

            def hidden(k, j, rounds, of):
                pe.wait_ge(onehotT_ready, k + 1)
                if past(k, 2):
                    pe.wait_ge(leaky_ready, k - 1)
                whole = hidden_ps[:, j % 2, :]
                for i in range(PER):
                    unit = slice(i * UNIT, (i + 1) * UNIT)
                    for s in range(3):
                        t.matmul(whole[:, unit], p_parts[:, bass.ds(of[i], 1), s, :].rearrange("p a f -> p (a f)"),
                                 onehotT[:, j % 3, unit], start=(s == 0), stop=False, skip_group_check=True)
                    if i == 0:
                        pe.wait_ge(gathered[j % U], rounds * (16 * C))
                    for c in range(i * UC, (i + 1) * UC):
                        mm = t.matmul(whole[:, c * P:(c + 1) * P], rows[:, j % U, c, 0:F], identf[:],
                                      start=False, stop=(c == (i + 1) * UC - 1), skip_group_check=True)
                mm.then_inc(hidden_done, 1)

            def mask(k, j):
                pe.wait_ge(leaky_ready, k + 1)
                if past(k, 2):
                    pe.wait_ge(weightsT_ready, k - 1)
                whole = masked_ps[:, j % 2, :]
                t.matmul(whole, other[:], onehotT[:, j % 3, :], start=True, stop=False)
                t.matmul(whole, w_cols[:], leaky[:, j % 2, :], start=False, stop=True).then_inc(masked_done, 1)

            def turn_weights(k, j):
                pe.wait_ge(weightsT_ready, k + 1)
                if past(k, 1):
                    pe.wait_ge(weights_ready, k)
                for c in range(C):
                    mm = t.transpose(weights_ps[:, c * P:(c + 1) * P], weightsT[:, j % 2, c * P:(c + 1) * P], identf[:])
                mm.then_inc(weights_done, 1)

            def chunk_sums(k, j):
                pe.wait_ge(weights_ready, k + 1)
                pe.wait_ge(ones_ready, k + 1)
                if past(k, 1):
                    pe.wait_ge(sums_ready, k * PER)
                for c in range(C):
                    mm = t.matmul(unit_sums_ps[:, c // UC, :], weights[:, j % 2, c * P:(c + 1) * P],
                                  rows[:, j % U, c, F:R], start=(c % UC == 0), stop=(c % UC == UC - 1))
                mm.then_inc(chunk_sums_done, 1)

            pe.wait_ge(blk_loaded, 32)
            pe.wait_ge(split, 1 + ALL_SPLITS)
            pe.wait_ge(w_cols_ready, 1)
            early = blocks_of(mybir.EngineType.PE, 0, 0, 4)
            for k in range(4):
                turn_onehot(k, k)
                hidden(k, k, 1, early[k * PER:(k + 1) * PER])
                if k >= 1:
                    mask(k - 1, k - 1)
            turn_weights(0, 0)

            def step(i, j, ahead):
                k = i * U + j
                turn_onehot(k + 4, j + 4)
                chunk_sums(k, j)
                turn_weights(k + 1, j + 1)
                hidden(k + 4, j + 4, i + 1 + (j + 4) // U, ahead[j * PER:(j + 1) * PER])
                mask(k + 3, j + 3)

            chunks(pe, step, lambda i: blocks_of(mybir.EngineType.PE, i, 4, U))

        @block.vector
        def _(dve):
            v = nc.vector
            v.memset(recv[96:P, REST:], NB * P).then_inc(filled, 1)
            v.memset(keys_i[96:P, :, :], PAD_ROW).then_inc(filled, 1)
            v.memset(x_sb[:, NB - 1, :], 0.0).then_inc(filled, 1)
            v.memset(bias3[:], 0.0).then_inc(filled, 1)
            v.memset(identf[:], 0.0).then_inc(filled, 1)
            v.memset(identb[:], 0.0).then_inc(filled, 1)
            v.memset(other[:], -BIG).then_inc(filled, 1)
            v.memset(onesf[:], 1.0).then_inc(filled, 1)
            v.memset(pad_row[:], 0.0).then_inc(filled, 1)
            v.memset(low_peak[:], 0.5 * BIG).then_inc(filled, 1)
            dve.wait_ge(consts, 5)
            v.tensor_copy(lane[:], lane_i[:]).then_inc(consts_v, 1)
            v.tensor_copy(unit_no[:], unit_i[:]).then_inc(consts_v, 1)
            v.tensor_scalar(thresholds[:], block_i[:], -1.0, 0.5, ALU.mult, ALU.add).then_inc(consts_v, 1)
            v.memset(signs[:, 0:1], float(T)).then_inc(signed, 1)
            for j in range(PHASES - LOCAL):
                v.tensor_scalar(bit_i[:, j:j + 1], part_i[:], j, 1, ALU.arith_shift_right,
                                ALU.bitwise_and).then_inc(consts_v, 1)
            v.tensor_scalar(past_edges[:], part_i[:], float(EDGE_ROWS), -2.0, ALU.is_ge, ALU.mult).then_inc(consts_v, 1)
            dve.wait_ge(consts_v, 4 + PHASES - LOCAL)
            v.tensor_scalar(sign_of[:], bit_i[:, 0:PHASES - LOCAL], -2.0, 1.0, ALU.mult, ALU.add).then_inc(consts_v, 1)
            v.tensor_tensor(tail_sign[:], past_edges[:], bit_i[:, 0:1], ALU.mult).then_inc(consts_v, 1)
            dve.wait_ge(consts_v, 6 + PHASES - LOCAL)
            v.tensor_scalar(tail_sign[:], tail_sign[:], 1.0, None, ALU.add).then_inc(consts_v, 1)

            dve.wait_ge(edges_in, 144)
            v.tensor_scalar(recv[:], recv[:], P.bit_length() - 1, None, ALU.arith_shift_right).then_inc(prepared, 1)
            dve.wait_ge(prepared, 1)
            v.tensor_copy(block_of[:], recv[:]).then_inc(prepared, 1)
            v.tensor_scalar(keys_i[:, 0, :], keys_i[:, 0, :], SENDER_BITS, MARK, ALU.logical_shift_left,
                            ALU.bitwise_or).then_inc(prepared, 1)
            dve.wait_ge(prepared, 3)
            v.tensor_tensor(keys_i[:, 0, :], keys_i[:, 0, :], keys_i[:, 1, :], ALU.bitwise_or).then_inc(prepared, 1)
            dve.wait_ge(prepared, 4)
            dve.wait_ge(consts_v, 7 + PHASES - LOCAL)
            v.tensor_scalar(keys[96:P, 0, :], keys[96:P, 0, :], tail_sign[96:P, :], None, ALU.mult).then_inc(prepared, 1)
            dve.wait_ge(prepared, 5)

            dve.wait_ge(weights_in, 7 * 16)
            dve.wait_ge(filled, FILLS)
            v.tensor_scalar(pad_row[:, 0:F], w_row[:], 0.0, -2.0 * LOW, ALU.is_gt, ALU.mult).then_inc(pad_row_ready, 1)
            dve.wait_ge(pad_row_ready, 1)
            v.tensor_scalar(pad_row[:, 0:F], pad_row[:, 0:F], LOW, None, ALU.add).then_inc(pad_row_ready, 2)
            v.tensor_scalar(w_cols[:], onesf[:], w_col[:], None, ALU.mult).then_inc(w_cols_ready, 1)

            def make_padding():
                dve.wait_ge(totals_ps, 1)
                v.tensor_copy(sign_sums[:], sums_ps[:, 0:NB + 1]).then_inc(based, 1)
                dve.wait_ge(based, 1)
                v.tensor_tensor(twice[:], sign_sums[:, 0:NB], sign_sums[:, 1:], ALU.subtract).then_inc(based, 1)
                dve.wait_ge(based, 2)
                v.tensor_scalar(edges_of[:], twice[:], 0.5, None, ALU.mult).then_inc(based, 1)
                v.tensor_scalar(nb_i[:], twice[:], 0.5, float(UNIT - 1), ALU.mult, ALU.add).then_inc(based, 1)
                dve.wait_ge(based, 4)
                v.tensor_scalar(nb_i[:], nb_i[:], UNIT.bit_length() - 1, None, ALU.arith_shift_right).then_inc(based, 1)
                dve.wait_ge(based, 5)
                v.tensor_copy(nb_f[:], nb_i[:]).then_inc(based, 1)
                dve.wait_ge(based, 6)
                v.tensor_tensor_scan(ends[:], nb_f[:], nb_f[:], 0.0, ALU.add, ALU.max).then_inc(based, 1)
                v.scalar_tensor_tensor(out=need[:], in0=nb_f[:], scalar=float(UNIT), in1=edges_of[:],
                                       op0=ALU.mult, op1=ALU.subtract).then_inc(based, 1)
                dve.wait_ge(based, 8)
                v.tensor_tensor_scan(need_ends[:], need[:], need[:], 0.0, ALU.add, ALU.max).then_inc(based, 1)
                v.tensor_tensor(passed[:], ends[:].unsqueeze(1).to_broadcast([P, SLOTS, NB]),
                                unit_no[:].unsqueeze(2).to_broadcast([P, SLOTS, NB]), ALU.is_le).then_inc(based, 1)
                dve.wait_ge(based, 10)
                v.tensor_reduce(blk_f[:], passed[:], AX_X, ALU.add).then_inc(based, 1)
                dve.wait_ge(based, 11)
                v.tensor_scalar(blk_i[:], blk_f[:], float(NB - 1), None, ALU.min).then_inc(blk_ready, 1)
                assert EDGE_ROWS % 2 == 1
                row_bit, col = pad_work[:, 0, :], pad_work[:, 1, :]
                v.tensor_scalar(row_bit, pad_i[:], LOCAL, 1, ALU.arith_shift_right, ALU.bitwise_and).then_inc(pad_steps, 1)
                v.tensor_scalar(col, pad_i[:], WIDTH - 1, None, ALU.bitwise_and).then_inc(pad_steps, 1)
                dve.wait_ge(pad_steps, 2)
                v.tensor_scalar(pad_up[:], col, -2.0, float(WIDTH - 1), ALU.mult, ALU.add).then_inc(pad_steps, 1)
                v.tensor_scalar(pad_turn[:], row_bit, -1.0, 1.0, ALU.mult, ALU.add).then_inc(pad_steps, 1)
                v.tensor_scalar(pad_sign[:], row_bit, 2.0, -1.0, ALU.mult, ALU.add).then_inc(pad_steps, 1)
                dve.wait_ge(pad_steps, 5)
                v.tensor_tensor(pad_up[:], pad_up[:], pad_turn[:], ALU.mult).then_inc(pad_steps, 1)
                dve.wait_ge(pad_steps, 6)
                v.tensor_tensor(pad_up[:], pad_up[:], pad_i[:], ALU.add).then_inc(pad_steps, 1)
                v.memset(pad_block[:], 0.0).then_inc(pad_steps, 1)
                dve.wait_ge(pad_steps, 8)
                def passes(b, i):
                    dve.wait_ge(pad_steps, b + 7)
                    v.scalar_tensor_tensor(out=pad_block[:, i, :], in0=pad_up[:], scalar=need_ends[:, bass.ds(b, 1)],
                                           in1=pad_block[:, i, :], op0=ALU.is_ge, op1=ALU.add).then_inc(pad_steps, 1)

                with dve.Fori(0, NB // 8) as eight:
                    for i in range(8):
                        passes(eight * 8 + i, i % 2)
                for b in range(NB // 8 * 8, NB):
                    passes(b, b % 2)
                dve.wait_ge(pad_steps, NB + 8)
                v.tensor_tensor(row_bit, pad_block[:, 0, :], pad_block[:, 1, :], ALU.add).then_inc(pad_steps, 1)
                dve.wait_ge(pad_steps, NB + 9)
                v.tensor_scalar(col, row_bit, SENDER_BITS + P.bit_length() - 1, MARK | PAD_ROW,
                                ALU.logical_shift_left, ALU.bitwise_or).then_inc(pad_steps, 1)
                dve.wait_ge(pad_steps, NB + 10)
                v.tensor_tensor(pad_turn[:], col.bitcast(F32), pad_sign[:], ALU.mult).then_inc(pads_ready, 1)

            def split_p(step):
                dve.wait_ge(split, 1 + sum(len(x) for x in SPLITS[:step]))
                for s, part in SPLITS[step]:
                    at = slice(s * BY, (s + 1) * BY)
                    v.tensor_tensor(p_f32[:, at, :], p_f32[:, at, :], p_parts[:, at, part, :],
                                    ALU.subtract).then_inc(lessened, 1)

            def compare(src, dst, dist):
                ins, outs = [x.rearrange("p (m t d) -> p m t d", t=2, d=dist) for x in (src, dst)]
                a, b = ins[:, :, 0, :], ins[:, :, 1, :]
                v.tensor_tensor(outs[:, :, 0, :], a, b, ALU.min)
                return v.tensor_tensor(outs[:, :, 1, :], a, b, ALU.max)

            def compare_groups(src, dst, dist, group, r):
                ins, outs = [x.rearrange("p (g r m t d) -> p g r m t d", r=2, m=group // (2 * dist), t=2, d=dist)
                             for x in (src, dst)]
                a, b = ins[:, :, r, :, 0, :], ins[:, :, r, :, 1, :]
                v.tensor_tensor(outs[:, :, r, :, r, :], a, b, ALU.min)
                return v.tensor_tensor(outs[:, :, r, :, 1 - r, :], a, b, ALU.max)

            done, now = 0, 0
            edge_rows = slice(0, EDGE_ROWS)
            for phase in range(1, LOCAL):
                if done:
                    dve.wait_ge(compared, done)
                for stage in reversed(range(phase)):
                    for r in (0, 1):
                        if stage < phase - 1:
                            dve.wait_ge(compared, done - 1)
                        compare_groups(keys[edge_rows, now, :], keys[edge_rows, 1 - now, :], 1 << stage,
                                       1 << phase, r).then_inc(compared, 1)
                        done += 1
                    now = 1 - now
            dve.wait_ge(compared, done)
            half = keys[edge_rows, now, :]
            v.tensor_scalar(half, half, sign_of[edge_rows, 0:1], None, ALU.mult).then_inc(compared, 1)
            done += 1

            def within(rows, now, done, between=None):
                small = LOCAL - 1
                dve.wait_ge(compared, done)
                compare(keys[rows, now, :], keys[rows, 1 - now, :], PIECE).then_inc(compared, 1)
                now, done = 1 - now, done + 1
                left = [done, done]
                for n in range(small + LEAD):
                    if n == LEAD + 2 and between:
                        between()
                    for h, stage in ((0, n), (1, n - LEAD)):
                        if 0 <= stage < small:
                            at = slice(h * PIECE, (h + 1) * PIECE)
                            side = (now + stage) % 2
                            dve.wait_ge(compared, left[h])
                            end = stage == small - 1
                            compare(keys[rows, side, at], keys[rows, 1 - side, at], PIECE >> (stage + 1)).then_inc(
                                run_done if end else compared, 1)
                            if not end:
                                done += 1
                                left[h] = done
                return done

            done = within(edge_rows, now, done, between=make_padding)
            for run in range(1, RUNS):
                phase, now = phase_of(run), starts_in[run]
                if run % 2:
                    stages = phase - LOCAL
                    groups = (0, 1) if phase < PHASES else (None,)
                    each = stages * len(groups) - 1
                    with dve.Fori(0, 2) as h:
                        side = [keys[:, n, bass.ds(h * PIECE, PIECE)] for n in (now, 1 - now)]
                        dve.wait_ge(turn_out, h + (2 * (run - 1) + 1))
                        for n in range(stages):
                            for i, r in enumerate(groups):
                                if n:
                                    dve.wait_ge(compared, h * each + (done + (n - 1) * len(groups) + i + 1))
                                args = side[n % 2], side[1 - n % 2], 1 << (stages - 1 - n)
                                last = compare(*args) if r is None else compare_groups(*args, 1 << stages, r)
                                last.then_inc(run_done if n == stages - 1 and r != 0 else compared, 1)
                    done += 2 * each
                    if run == RUNS - 1:
                        dve.wait_ge(run_done, 2 * RUNS)
                        now = (now + stages) % 2
                        for stage in range(LOCAL - 1, UNIT.bit_length() - 2, -1):
                            if stage < LOCAL - 1:
                                dve.wait_ge(compared, done)
                            compare(keys[:, now, :], keys[:, 1 - now, :], 1 << stage).then_inc(compared, 1)
                            now, done = 1 - now, done + 1
                else:
                    split_p(run // 2 - 1)
                    dve.wait_ge(turn_out, 2 * run)
                    done = within(slice(0, P), now, done)

            dve.wait_ge(compared, done)
            by_tile = dict(q=P)
            bits = keys_i[:, ends_in[-1], :].rearrange("p (c q) -> p q c", **by_tile)
            raw = lane_bits.rearrange("p (q c) -> p q c", **by_tile)
            who = senders[:].rearrange("p (q c) -> p q c", **by_tile)
            lane_at = lanes[:].rearrange("p (q c) -> p q c", **by_tile)
            TILES = WIDTH // P
            FIRST, USED = 16 * C // TILES, -(-(NCH + U + 2) * C // TILES)
            for s, q in enumerate((slice(0, FIRST), slice(FIRST, USED))):
                v.tensor_scalar(who[:, q, :], bits[:, q, :], (1 << SENDER_BITS) - 1, None,
                                ALU.bitwise_and).then_inc(unpacked, 1)
                v.tensor_scalar(raw[:, q, :], bits[:, q, :], SENDER_BITS, P - 1, ALU.arith_shift_right,
                                ALU.bitwise_and).then_inc(unpacked, 1)
                dve.wait_ge(unpacked, 4 * s + 2)
                v.tensor_scalar(lane_at[:, q, :], who[:, q, :], float(PAD_ROW), float(P), ALU.is_ge,
                                ALU.mult).then_inc(unpacked, 1)
                dve.wait_ge(unpacked, 4 * s + 3)
                v.tensor_tensor(lane_at[:, q, :], lane_at[:, q, :], raw[:, q, :], ALU.add).then_inc(unpacked, 1)
            dve.wait_ge(unpacked, 8)
            dve.wait_ge(blk_loaded, 32)
            dve.wait_ge(cleared, 1)

            def make_onehot(k, j):
                if past(k, 2):
                    dve.wait_ge(onehotT_done, k - 1)
                v.tensor_tensor(onehot[:, j % 2], lane[:].unsqueeze(1).to_broadcast([P, C, P]),
                                lanes[:, bass.ds(k * C, C)].unsqueeze(2).to_broadcast([P, C, P]),
                                ALU.is_equal).then_inc(onehot_ready, 1)

            def leaky_relu(k, j):
                dve.wait_ge(sloped_ready, k + 1)
                if past(k, 2):
                    dve.wait_ge(masked_done, k - 1)
                v.tensor_tensor(leaky[:, j % 2, :], hidden_ps[:, j % 2, :], sloped[:, j % 2, :],
                                ALU.max).then_inc(leaky_ready, 1)

            def mark_ones(k, j):
                if past(k, U):
                    dve.wait_ge(chunk_sums_done, k - U + 1)
                v.tensor_scalar(rows[:, j % U, :, 2 * F], lanes[:, bass.ds(k * C, C)], float(P), None,
                                ALU.is_lt).then_inc(ones_ready, 1)

            def lowest(k, j):
                dve.wait_ge(masked_done, k + 1)
                if past(k, 1):
                    dve.wait_ge(new_low_ready, k * PER)
                v.tensor_reduce(unit_low[:], masked_ps[:, j % 2, :].rearrange("p (i e) -> p i e", i=PER), AX_X,
                                ALU.max, negate=True).then_inc(unit_low_ready, 1)

            def new_peak(k, j, i, of):
                dve.wait_ge(unit_low_ready, k + 1)
                if past(k, 2):
                    dve.wait_ge(weightsT_ready, k - 1)
                if past(k, 1) or i:
                    dve.wait_ge(peak_ready, k * PER + i)
                v.tensor_tensor(new_low[:, j % 2, i:i + 1], unit_low[:, i:i + 1], low_peak[:, bass.ds(of[i], 1)],
                                ALU.min).then_inc(new_low_ready, 1)

            def grow(k, j, i, of):
                dve.wait_ge(new_low_ready, k * PER + i + 1)
                if past(k, 2):
                    dve.wait_ge(shrink_ready, k - 1)
                v.tensor_tensor(growth[:, j % 2, i:i + 1], new_low[:, j % 2, i:i + 1], low_peak[:, bass.ds(of[i], 1)],
                                ALU.subtract).then_inc(growth_ready, 1)

            def set_peak(k, j, i, of):
                dve.wait_ge(growth_ready, k * PER + i + 1)
                new = new_low[:, j % 2, i:i + 1]
                v.tensor_tensor(low_peak[:, bass.ds(of[i], 1)], new, new, ALU.min).then_inc(peak_ready, 1)

            def add_sums(k, j, i, of):
                dve.wait_ge(chunk_sums_done, k + 1)
                dve.wait_ge(shrink_ready, k + 1)
                if past(k, 1) or i:
                    dve.wait_ge(sums_ready, k * PER + i)
                at = sums[:, bass.ds(of[i], 1), :].rearrange("p a f -> p (a f)")
                v.scalar_tensor_tensor(out=at, in0=at, scalar=shrink[:, j % 2, i:i + 1], in1=unit_sums_ps[:, i, :],
                                       op0=ALU.mult, op1=ALU.add).then_inc(sums_ready, 1)

            def raise_peak(k, of):
                lowest(k, k)
                for i in range(PER):
                    for part in (new_peak, grow, set_peak):
                        part(k, k, i, of)

            early = blocks_of(mybir.EngineType.DVE, 0, 0, 2)
            make_onehot(0, 0)
            make_onehot(1, 1)
            leaky_relu(0, 0)
            make_onehot(2, 2)
            leaky_relu(1, 1)
            for k in (0, 1):
                raise_peak(k, early[k * PER:(k + 1) * PER])
                mark_ones(k, k)
                make_onehot(k + 3, k + 3)
                if k == 0:
                    leaky_relu(2, 2)

            def step(i, j, of):
                k = i * U + j
                now, later = of[j * PER:(j + 1) * PER], of[(j + 2) * PER:(j + 3) * PER]
                lowest(k + 2, j + 2)
                make_onehot(k + 5, j + 5)
                new_peak(k + 2, j + 2, 0, later)
                mark_ones(k + 2, j + 2)
                grow(k + 2, j + 2, 0, later)
                leaky_relu(k + 3, j + 3)
                set_peak(k + 2, j + 2, 0, later)
                add_sums(k, j, 0, now)
                new_peak(k + 2, j + 2, 1, later)
                add_sums(k, j, 1, now)
                grow(k + 2, j + 2, 1, later)
                set_peak(k + 2, j + 2, 1, later)

            chunks(dve, step, lambda i: blocks_of(mybir.EngineType.DVE, i, 0, U + 2))

            dve.wait_ge(sums_ready, NCH * PER)
            v.tensor_scalar(recip[:], sums[:, :, F], 1e-12, None, ALU.max).then_inc(finish, 1)
            dve.wait_ge(finish, 1)
            v.reciprocal(recip[:], recip[:]).then_inc(finish, 1)
            dve.wait_ge(finish, 2)
            for g in range(SLICES):
                at = slice(g * BY, (g + 1) * BY)
                n = sums[:, at, 0:F]
                v.tensor_tensor(n, n, recip[:, at].unsqueeze(2).to_broadcast([P, BY, F]), ALU.mult).then_inc(divided, 1)
            dve.wait_ge(x_less, 1)
            for n, (first, end) in enumerate(BATCHES):
                for g in range(first, end):
                    at = slice(g * BY, (g + 1) * BY)
                    y = x_sb[:, at, :]
                    dve.wait_ge(exp_done, g + 1)
                    v.scalar_tensor_tensor(out=y, in0=elu_work[:, at, :], scalar=1.0, in1=y,
                                           op0=ALU.min, op1=ALU.add).then_inc(mixed, 1)
                    dve.wait_ge(mixed, 2 * g + 1)
                    v.scalar_tensor_tensor(out=y, in0=sums[:, at, 0:F], scalar=0.0, in1=y,
                                           op0=ALU.max, op1=ALU.add).then_inc(mixed, 1)
                    dve.wait_ge(mixed, 2 * g + 2)
                    for b in range(g * BY, (g + 1) * BY):
                        last = v.bn_stats(stats[:, b, :], x_sb[:, b, :])
                    last.then_inc(measured, 1)
                    dve.wait_ge(measured, 2 * g + 1)
                    for b in range(g * BY, (g + 1) * BY):
                        last = v.bn_aggr(moments[:, b, :], stats[:, b, :])
                    last.then_inc(measured, 1)
                at = slice(first * BY, end * BY)
                dve.wait_ge(measured, 2 * end)
                v.tensor_scalar(recip[:, at], moments[:, at, 1], EPS, None, ALU.add).then_inc(spread, 1)
                dve.wait_ge(sqrt_done, n + 1)
                v.reciprocal(recip[:, at], recip[:, at]).then_inc(spread, 1)
                dve.wait_ge(spread, 3 * n + 2)
                v.scalar_tensor_tensor(out=offset[:, at], in0=moments[:, at, 0], scalar=-1.0, in1=recip[:, at],
                                       op0=ALU.mult, op1=ALU.mult).then_inc(spread, 1)
            for b in range(NB - LAST_V, NB):
                v.tensor_scalar(x_sb[:, b, :], x_sb[:, b, :], moments[:, b, 0:1], recip[:, b:b + 1],
                                ALU.subtract, ALU.mult).then_inc(normed_v, 1)


_INS = ["x", "src", "dst", "L0_gnn_W_lin", "L0_gnn_b_lin", "L0_gnn_W_att", "L0_gnn_b_att", "L0_gnn_w_alpha"]


def kernel(**inputs):
    import numpy as _np
    import concourse.bacc as _bacc
    from concourse import mybir as _mybir
    from concourse.bass_utils import run_bass_kernel_spmd as _run

    nc = _bacc.Bacc("TRN2", target_bir_lowering=False, num_devices=1)
    arrays, args = {}, []
    for name in _INS:
        a = _np.ascontiguousarray(inputs[name])
        arrays[f"in_{name}"] = a
        args.append(nc.dram_tensor(f"in_{name}", a.shape, _mybir.dt.from_np(a.dtype), kind="ExternalInput").ap())
    shape = inputs["x"].shape
    args.append(nc.dram_tensor("out_0", shape, F32, kind="ExternalOutput").ap())
    gnn_kernel(nc, *args)
    r = _run(nc, [arrays], core_ids=[0])
    return r.results[0]["out_0"]
```
